# Optimizing a Trainium2 kernel written in Bass

```python
import numpy as np
import jax
import jax.numpy as jnp

def _softmax(x, axis=-1):
    return jax.nn.softmax(x, axis=axis)

def _gelu(x):
    return jax.nn.gelu(x, approximate=True)

def _silu(x):
    return jax.nn.silu(x)

def _sigmoid(x):
    return jax.nn.sigmoid(x)

def _layernorm(x, axis=-1, eps=1e-05):
    m = jnp.mean(x, axis=axis, keepdims=True)
    v = jnp.var(x, axis=axis, keepdims=True)
    return (x - m) / jnp.sqrt(v + eps)

def _scatter_add(tgt, idx, src, axis=0):
    return tgt.at[idx].add(src)

def _segment_sum(src, seg, n):
    return jax.ops.segment_sum(src, seg, n)
kernel_name = 'mk_early_fusion_d1_tok_img1024_r4_b84700'

def setup_inputs(seed: int=0):
    np.random.seed(seed)
    _w = jnp.asarray

    def _rec_inputs():
        import jax
        import jax.numpy as jnp
        _rk = jax.random.key(seed)
        x = -0.00016672 + 0.999947 * jax.random.normal(jax.random.fold_in(_rk, 1), (32, 3, 96, 96), jnp.float32)
        txt = -1.44135e-05 + 0.554504 * jax.random.normal(jax.random.fold_in(_rk, 2), (32, 32, 256), jnp.float32)
        return (x, txt)
    x, txt = _rec_inputs()

    def _L0_tok_setup():
        import jax, jax.numpy as jnp
        import numpy as np
        P = 16

        def _patchify(x):
            B, C, H, W = x.shape
            gh, gw = (H // P, W // P)
            x = x.reshape(B, C, gh, P, gw, P)
            x = x.transpose(0, 2, 4, 1, 3, 5)
            return x.reshape(B, gh * gw, C * P * P)
        key = jax.random.key(seed)
        k1, k2, k3, k4, k5 = jax.random.split(key, 5)
        B, C, S = (64, 3, 96)
        lin_in, lout = (P * P * C, 256)
        n_patches = (S // P) ** 2
        return {'x': jax.random.normal(k1, (B, C, S, S), dtype=jnp.float32), 'W': jax.random.normal(k2, (lout, lin_in), dtype=jnp.float32) * 0.02, 'b': jax.random.normal(k3, (lout,), dtype=jnp.float32) * 0.02, 'class_token': jax.random.normal(k4, (1, 1, lout), dtype=jnp.float32) * 0.02, 'pos_embedding': jax.random.normal(k5, (1, n_patches + 1, lout), dtype=jnp.float32) * 0.02}
    _L0_tok_all = _L0_tok_setup()
    _L0_tok_in = {k: v for k, v in _L0_tok_all.items() if k in ('W', 'b', 'class_token', 'pos_embedding')}
    del _L0_tok_all

    def _L0_attn_setup():
        import jax, jax.numpy as jnp
        import numpy as np
        B, T, C = (2, 512, 256)
        LAT = 64
        N_HEAD = 16
        HEAD_DIM = C // N_HEAD
        SCALE = 1.0 / np.sqrt(HEAD_DIM).astype(np.float32)
        key = jax.random.key(seed)
        ks = jax.random.split(key, 9)
        s_in = 0.02
        return {'x': jax.random.normal(ks[0], (B, T, C), dtype=jnp.float32), 'wq_lat': jax.random.normal(ks[1], (C, LAT), dtype=jnp.float32) * s_in, 'wk_lat': jax.random.normal(ks[2], (C, LAT), dtype=jnp.float32) * s_in, 'wv_lat': jax.random.normal(ks[3], (C, LAT), dtype=jnp.float32) * s_in, 'wq_heads': jax.random.normal(ks[4], (LAT, C), dtype=jnp.float32) * s_in, 'wk_heads': jax.random.normal(ks[5], (LAT, C), dtype=jnp.float32) * s_in, 'wv_heads': jax.random.normal(ks[6], (LAT, C), dtype=jnp.float32) * s_in, 'w_proj': jax.random.normal(ks[7], (C, C), dtype=jnp.float32) * s_in, 'b_proj': jnp.zeros((C,), dtype=jnp.float32)}
    _L0_attn_all = _L0_attn_setup()
    _L0_attn_in = {k: v for k, v in _L0_attn_all.items() if k in ('wq_lat', 'wk_lat', 'wv_lat', 'wq_heads', 'wk_heads', 'wv_heads', 'w_proj', 'b_proj')}
    del _L0_attn_all

    def _L0_ffn_setup():
        import jax, jax.numpy as jnp
        import numpy as np
        B, S, D, H, E = (64, 256, 256, 64, 8)
        EPS = 1e-05
        key = jax.random.key(seed)
        ks = jax.random.split(key, 8)
        x = jax.random.normal(ks[0], (B, S, D), jnp.float32)
        return {'x': x, 'ln_g': jnp.ones((D,), jnp.float32), 'ln_b': jnp.zeros((D,), jnp.float32), 'bn_g': jnp.ones((D,), jnp.float32), 'bn_b': jnp.zeros((D,), jnp.float32), 'bn_mean': jax.random.normal(ks[1], (D,), jnp.float32) * 0.01, 'bn_var': jnp.ones((D,), jnp.float32), 'Wr': jax.random.normal(ks[2], (D, E), jnp.float32) * 0.02, 'br': jnp.zeros((E,), jnp.float32), 'W_down': jax.random.normal(ks[3], (E, D, H), jnp.float32) * 0.02, 'b_down': jnp.zeros((E, H), jnp.float32), 'W_up': jax.random.normal(ks[4], (E, H, D), jnp.float32) * 0.02, 'b_up': jnp.zeros((E, D), jnp.float32)}
    _L0_ffn_all = _L0_ffn_setup()
    _L0_ffn_in = {k: v for k, v in _L0_ffn_all.items() if k in ('ln_g', 'ln_b', 'bn_g', 'bn_b', 'bn_mean', 'bn_var', 'Wr', 'br', 'W_down', 'b_down', 'W_up', 'b_up')}
    del _L0_ffn_all
    return {'x': x, 'txt': txt, 'L0_tok_W': _L0_tok_in['W'], 'L0_tok_b': _L0_tok_in['b'], 'L0_tok_class_token': _L0_tok_in['class_token'], 'L0_tok_pos_embedding': _L0_tok_in['pos_embedding'], 'L0_attn_wq_lat': _L0_attn_in['wq_lat'], 'L0_attn_wk_lat': _L0_attn_in['wk_lat'], 'L0_attn_wv_lat': _L0_attn_in['wv_lat'], 'L0_attn_wq_heads': _L0_attn_in['wq_heads'], 'L0_attn_wk_heads': _L0_attn_in['wk_heads'], 'L0_attn_wv_heads': _L0_attn_in['wv_heads'], 'L0_attn_w_proj': _L0_attn_in['w_proj'], 'L0_attn_b_proj': _L0_attn_in['b_proj'], 'L0_ffn_ln_g': _L0_ffn_in['ln_g'], 'L0_ffn_ln_b': _L0_ffn_in['ln_b'], 'L0_ffn_bn_g': _L0_ffn_in['bn_g'], 'L0_ffn_bn_b': _L0_ffn_in['bn_b'], 'L0_ffn_bn_mean': _L0_ffn_in['bn_mean'], 'L0_ffn_bn_var': _L0_ffn_in['bn_var'], 'L0_ffn_Wr': _L0_ffn_in['Wr'], 'L0_ffn_br': _L0_ffn_in['br'], 'L0_ffn_W_down': _L0_ffn_in['W_down'], 'L0_ffn_b_down': _L0_ffn_in['b_down'], 'L0_ffn_W_up': _L0_ffn_in['W_up'], 'L0_ffn_b_up': _L0_ffn_in['b_up']}

def reference(x, txt, L0_tok_W, L0_tok_b, L0_tok_class_token, L0_tok_pos_embedding, L0_attn_wq_lat, L0_attn_wk_lat, L0_attn_wv_lat, L0_attn_wq_heads, L0_attn_wk_heads, L0_attn_wv_heads, L0_attn_w_proj, L0_attn_b_proj, L0_ffn_ln_g, L0_ffn_ln_b, L0_ffn_bn_g, L0_ffn_bn_b, L0_ffn_bn_mean, L0_ffn_bn_var, L0_ffn_Wr, L0_ffn_br, L0_ffn_W_down, L0_ffn_b_down, L0_ffn_W_up, L0_ffn_b_up):
    import jax
    import jax.numpy as jnp

    def _L0_tok_ref(x, W, b, class_token, pos_embedding):
        import jax, jax.numpy as jnp
        import numpy as np
        P = 16

        def _patchify(x):
            B, C, H, W = x.shape
            gh, gw = (H // P, W // P)
            x = x.reshape(B, C, gh, P, gw, P)
            x = x.transpose(0, 2, 4, 1, 3, 5)
            return x.reshape(B, gh * gw, C * P * P)
        patches = _patchify(x)
        proj = jnp.einsum('bnk,dk->bnd', patches, W) + b
        B = x.shape[0]
        cls = jnp.broadcast_to(class_token, (B, 1, proj.shape[-1]))
        out = jnp.concatenate([cls, proj], axis=1) + pos_embedding
        return out

    def _L0_attn_ref(x, wq_lat, wk_lat, wv_lat, wq_heads, wk_heads, wv_heads, w_proj, b_proj):
        import jax, jax.numpy as jnp
        import numpy as np
        B, T, C = (2, 512, 256)
        LAT = 64
        N_HEAD = 16
        HEAD_DIM = C // N_HEAD
        SCALE = 1.0 / np.sqrt(HEAD_DIM).astype(np.float32)
        Bx, Tx, Cx = x.shape
        q = x @ wq_lat @ wq_heads
        k = x @ wk_lat @ wk_heads
        v = x @ wv_lat @ wv_heads
        q = q.reshape(Bx, Tx, N_HEAD, HEAD_DIM).transpose(0, 2, 1, 3)
        k = k.reshape(Bx, Tx, N_HEAD, HEAD_DIM).transpose(0, 2, 1, 3)
        v = v.reshape(Bx, Tx, N_HEAD, HEAD_DIM).transpose(0, 2, 1, 3)
        att = jnp.einsum('bhqd,bhkd->bhqk', q, k) * SCALE
        causal = jnp.tril(jnp.ones((Tx, Tx), dtype=bool))
        att = jnp.where(causal[None, None], att, -jnp.inf)
        att = jax.nn.softmax(att, axis=-1)
        y = jnp.einsum('bhqk,bhkd->bhqd', att, v)
        y = y.transpose(0, 2, 1, 3).reshape(Bx, Tx, Cx)
        return y @ w_proj + b_proj

    def _L0_ffn_ref(x, ln_g, ln_b, bn_g, bn_b, bn_mean, bn_var, Wr, br, W_down, b_down, W_up, b_up):
        import jax, jax.numpy as jnp
        import numpy as np
        B, S, D, H, E = (64, 256, 256, 64, 8)
        EPS = 1e-05
        mu = jnp.mean(x, axis=-1, keepdims=True)
        var = jnp.var(x, axis=-1, keepdims=True)
        z = (x - mu) * jax.lax.rsqrt(var + EPS) * ln_g + ln_b
        z_sent = jnp.mean(z, axis=1)
        z_bn = (z_sent - bn_mean) * jax.lax.rsqrt(bn_var + EPS) * bn_g + bn_b
        probs = jax.nn.softmax(z_bn @ Wr + br, axis=-1)
        idx = jnp.argmax(probs, axis=-1)
        gate = jnp.take_along_axis(probs, idx[:, None], axis=1)[:, 0]
        h = jax.nn.relu(jnp.einsum('bsd,bdh->bsh', z, W_down[idx]) + b_down[idx][:, None, :])
        y = jnp.einsum('bsh,bhd->bsd', h, W_up[idx]) + b_up[idx][:, None, :]
        return y * gate[:, None, None]
    h = _L0_tok_ref(x, L0_tok_W, L0_tok_b, L0_tok_class_token, L0_tok_pos_embedding)
    h = jnp.concatenate([h, txt], axis=1)
    h = h + _L0_attn_ref(_layernorm(h, axis=-1), L0_attn_wq_lat, L0_attn_wk_lat, L0_attn_wv_lat, L0_attn_wq_heads, L0_attn_wk_heads, L0_attn_wv_heads, L0_attn_w_proj, L0_attn_b_proj)
    h = h + _L0_ffn_ref(_layernorm(h, axis=-1), L0_ffn_ln_g, L0_ffn_ln_b, L0_ffn_bn_g, L0_ffn_bn_b, L0_ffn_bn_mean, L0_ffn_bn_var, L0_ffn_Wr, L0_ffn_br, L0_ffn_W_down, L0_ffn_b_down, L0_ffn_W_up, L0_ffn_b_up)
    return h

_drawn_inputs = setup_inputs


def setup_inputs(seed=0):
    import zlib

    import numpy as np

    out = dict(_drawn_inputs(seed))
    spreads = {'L0_attn_b_proj': (0.0, 0.347),
     'L0_ffn_ln_g': (1.0, 0.6),
     'L0_ffn_ln_b': (0.0, 0.33),
     'L0_ffn_bn_g': (1.0, 0.6),
     'L0_ffn_bn_b': (0.0, 0.8),
     'L0_ffn_bn_var': (1.0, 0.6),
     'L0_ffn_br': (0.0, 0.1),
     'L0_ffn_b_down': (0.0, 2.0),
     'L0_ffn_b_up': (0.0, 2.0)}
    factors = {'L0_tok_class_token': 8.0,
     'L0_attn_wq_lat': 8.0,
     'L0_attn_wk_lat': 8.0,
     'L0_attn_wv_lat': 7.645,
     'L0_attn_wq_heads': 8.0,
     'L0_attn_wk_heads': 8.0,
     'L0_attn_wv_heads': 7.895,
     'L0_attn_w_proj': 7.928,
     'L0_ffn_bn_mean': 8.0,
     'L0_ffn_W_down': 6.095,
     'L0_ffn_W_up': 4.874}
    for name, (base, spread) in spreads.items():
        noise = np.random.default_rng([zlib.crc32(name.encode()), seed]).standard_normal(out[name].shape)
        drawn = base * np.exp(spread * noise) if base else spread * noise
        out[name] = jnp.asarray(drawn.astype(out[name].dtype))
    for name, factor in factors.items():
        out[name] = (out[name] * factor).astype(out[name].dtype)
    return out
```

```python
from contextlib import ExitStack

import numpy as np

import concourse.bass as bass
from concourse import mybir

ALU = mybir.AluOpType
ACT = mybir.ActivationFunctionType
F32 = mybir.dt.float32
BF16 = mybir.dt.bfloat16
I32 = mybir.dt.int32
U32 = mybir.dt.uint32
AX_X = mybir.AxisListType.X
ds = bass.ds

P = 128
B = 32
NPATCH, NTXT = 36, 32
T = 1 + NPATCH + NTXT
TP = T + 1
C = 256
KC = C // P
KX = 3 * 16 * 16 // P
RT = 4
NPT, NTT = NPATCH // RT, NTXT // RT
NT = NPT + NTT
HEADS, HD, LAT = 16, 16, 64
HH = P // HD
QB, NQ = 14, TP // 14
ROWS = HH * QB
G = 4
GN = G * TP
NG = B // G
EXPERTS, HID = 8, 64
VW = HD + 1
EPS = 1e-5
NEG = -1e30
WPK = KC * HID + C + 1


def width(i):
    return QB * (i + 1)


def offset(i):
    return QB * i * (i + 1)


def early_fusion(nc, patches, wtok, txt, pos_rows, tok_b, cls_tok, pos_cls, w_lat_qv, w_lat_k, w_heads_q,
                 w_heads_k, w_heads_v, w_proj, b_proj, cols, w_router, b_router, experts, causal, out):
    with ExitStack() as ctx:
        def sb(name, shape, dt=F32):
            return ctx.enter_context(nc.sbuf_tensor(name, shape, dt))

        def sem(name):
            return ctx.enter_context(nc.semaphore(name))

        ident = sb("ident", [P, P])
        ident_bf = sb("ident_bf", [ROWS, ROWS], BF16)
        mask = sb("mask", [ROWS, offset(NQ)], BF16)
        head_of_row = sb("head_of_row", [P, HH])
        seq_of_row = sb("seq_of_row", [P, B])
        h0 = sb("h0", [P, NT, C])
        h0c = sb("h0c", [B, C])
        xT = sb("xT", [P, KC, B * TP])
        qT = sb("qT", [P, KC, B * TP])
        kT = sb("kT", [P, KC, B * TP])
        yT = sb("yT", [P, KC, B * TP])
        v = sb("v", [TP, B, HEADS, VW])
        zT, h1T = xT, qT
        oT = kT[:, :, :].rearrange("p k n -> p (k n)")[:, 0:NG * KC * G * T]\
            .rearrange("p (g k n) -> p g k n", g=NG, k=KC)
        wlqv = sb("wlqv", [P, KC, P])
        wlk = sb("wlk", [P, KC, P])
        whq = sb("whq", [LAT, C])
        whk = sb("whk", [LAT, C])
        whv = sb("whv", [P, C])
        latqv = sb("latqv", [P, GN])
        latk = sb("latk", [P, GN])
        wp = sb("wp", [P, KC, C])
        bp = sb("bp", [P, C])
        tokb = sb("tokb", [P, C])
        colp = sb("colp", [P, 6, KC])
        eps_col = sb("eps_col", [P, 1])
        eps2_col = sb("eps2_col", [P, 1])
        bn_scale = sb("bn_scale", [P, KC])
        bn_tmp = sb("bn_tmp", [P, KC])
        zs_scale = sb("zs_scale", [P, KC])
        zs_shift = sb("zs_shift", [P, KC])
        wr = sb("wr", [P, KC, EXPERTS])
        br = sb("br", [B, EXPERTS])
        wall = sb("wall", [P, EXPERTS, WPK])
        wsel = sb("wsel", [P, G, WPK])
        hid = sb("hid", [HID + 1, G, T])
        xh = sb("xh", [P, 3, 2, C])
        xhc = sb("xhc", [B, C])
        st = sb("st", [P, 3, 2, 6])
        mv = sb("mv", [P, 3, 2, 2])
        sd = sb("sd", [P, 3, 2])
        rs = sb("rs", [P, 3, 2])
        ytile = sb("ytile", [P, 2, KC, P])
        h1 = sb("h1", [P, 2, C])
        zh = sb("zh", [P, 2, C])
        area = sb("area", [P, KX * C + 3 * KX * P + NPT * C])
        wt = area[:, 0:KX * C].rearrange("p (k n) -> p k n", k=KX)
        xin = area[:, KX * C:KX * C + 3 * KX * P].rearrange("p (s k n) -> p s k n", s=3, k=KX)
        posb = area[:, KX * C + 3 * KX * P:].rearrange("p (j n) -> p j n", j=NPT)
        n_q, n_d, n_p = 2 * HEADS * TP, 2 * 2 * NQ * TP, 2 * HEADS * TP
        qblk = area[:, 0:n_q].rearrange("p (s f i h q) -> p s f i h q", s=2, f=2, i=NQ, h=HH)
        dif = area[0:ROWS, n_q:n_q + n_d].rearrange("p (s f i n) -> p s f i n", s=2, f=2, i=NQ)
        prob = area[0:TP, n_q + n_d:n_q + n_d + n_p].rearrange("p (s h n) -> p s h n", s=2, h=HEADS)
        maskf = h1[0:ROWS, :, :].rearrange("p s n -> p (s n)")[:, 0:offset(NQ)]
        mx = sb("mx", [ROWS, 2, NQ, 2])
        rc = sb("rc", [TP, 2, HEADS])
        yn = sb("yn", [TP, 2, C])
        zbn = sb("zbn", [P, KC, B])
        lg = sb("lg", [B, EXPERTS])
        top = sb("top", [B, 8])
        ntop = sb("ntop", [B, 1])
        ex = sb("ex", [B, EXPERTS])
        exs = sb("exs", [B, 1])
        exr = sb("exr", [B, 1])
        pr = sb("pr", [B, EXPERTS])
        ptop = sb("ptop", [B, 8])
        pidx = sb("pidx", [B, 8], U32)
        gate_col = sb("gate_col", [B, P])
        idx_col = sb("idx_col", [B, 1])
        gate = sb("gate", [P, B])
        idx = sb("idx", [1, B], I32)
        ps = ctx.enter_context(nc.psum_tensor("ps", [P, 8, 512], F32))

        l_wt, l_txt, l_pos, l_tokb, l_cls = (sem(n) for n in ("l_wt", "l_txt", "l_pos", "l_tokb", "l_cls"))
        l_x = [sem(f"l_x{t}") for t in range(3)]
        l_wattn, l_wproj, l_cols, l_wall, l_mask = (sem(n) for n in
                                                    ("l_wattn", "l_wproj", "l_cols", "l_wall", "l_mask"))
        consts, posb_done, bproj_done = sem("consts"), sem("posb_done"), sem("bproj_done")
        mask_done, dif_init, hid_ones = sem("mask_done"), sem("dif_init"), sem("hid_ones")
        patch_mm, h_added, stats_a, aggr_a, sqrt_a, recip_a, norm_a, xpose_a, xT_done = (
            sem(n) for n in ("patch_mm", "h_added", "stats_a", "aggr_a", "sqrt_a", "recip_a", "norm_a",
                             "xpose_a", "xT_done"))
        cls_dve, cls_sqrt, cls_x, bn_dve = sem("cls_dve"), sem("cls_sqrt"), sem("cls_x"), sem("bn_dve")
        latqv_mm, latk_mm, latqv_cp, latk_cp, v_mm, q_mm, k_mm, q_cp, k_cp, v_cpa, v_cpd = (
            sem(n) for n in ("latqv_mm", "latk_mm", "latqv_cp", "latk_cp", "v_mm", "q_mm", "k_mm", "q_cp",
                             "k_cp", "v_cpa", "v_cpd"))
        qblk_done, score_mm, max_done, sub_done, prob_xp, exp_done, pv_mm, rec_done, ynorm, yT_xp, yT_cp = (
            sem(n) for n in ("qblk_done", "score_mm", "max_done", "sub_done", "prob_xp", "exp_done", "pv_mm",
                             "rec_done", "ynorm", "yT_xp", "yT_cp"))
        ytile_cp, proj_mm, h1_done, stats_c, aggr_c, sqrt_c, recip_c, zh_done, xpose_c, zT_cp, h1T_cp = (
            sem(n) for n in ("ytile_cp", "proj_mm", "h1_done", "stats_c", "aggr_c", "sqrt_c", "recip_c",
                             "zh_done", "xpose_c", "zT_cp", "h1T_cp"))
        r_dve, r_act, r_logit, r_bcast = sem("r_dve"), sem("r_act"), sem("r_logit"), sem("r_bcast")
        wsel_cp, down_mm, relu_done, up_mm, out_done, stored = (
            sem(n) for n in ("wsel_cp", "down_mm", "relu_done", "up_mm", "out_done", "stored"))

        FILLED, IDENTITIES, PADDING, V_ONES = 6, 8, 13, 14

        block = ctx.enter_context(nc.Block())

        @block.sync
        def _(sp):
            def load_patch(j, t):
                sp.dma_start(xin[:, t, :, :], patches[j, :, :, :]).then_inc(l_x[t], 16)

            load_patch(0, 0)
            sp.dma_start(wt[:, KX // 2:KX, :], wtok[:, KX // 2:KX, :]).then_inc(l_wt, 16)
            load_patch(1, 1)
            load_patch(2, 2)
            sp.dma_start(tokb[:, :], tok_b).then_inc(l_tokb, 16)
            sp.dma_start(posb, pos_rows).then_inc(l_pos, 16)
            for j in range(3, NPT):
                sp.wait_ge(patch_mm, j - 2)
                load_patch(j, j % 3)
            sp.dma_start(wall[:, :, :], experts).then_inc(l_wall, 16)
            with sp.Fori(0, NG) as i:
                sp.wait_ge(out_done, i * G + G)
                sp.dma_start(out[ds(i, 1), :, :].rearrange("o p n -> (o p) n"),
                             oT[:, ds(i, 1), :, :].rearrange("p o k n -> p (o k n)")).then_inc(stored, 16)
            sp.wait_ge(stored, 16 * NG)

        @block.gpsimd
        def _(pool):
            pool.memset(ident[:, :], 0.0).then_inc(consts, 1)
            pool.memset(ident_bf[:, :], 0.0).then_inc(consts, 1)
            pool.memset(head_of_row[:, :], 1.0).then_inc(consts, 1)
            pool.memset(seq_of_row[:, :], 1.0).then_inc(consts, 1)
            pool.memset(eps_col[:, :], EPS).then_inc(consts, 1)
            pool.memset(eps2_col[:, :], EPS * EPS).then_inc(consts, 1)
            pool.wait_ge(consts, FILLED)
            for m, n in ((ident, P), (ident_bf, ROWS)):
                pool.affine_select(out=m[:, :], in_=m[:, :], compare_op=ALU.not_equal, fill=1.0, base=0,
                                   pattern=[[-1, n]], channel_multiplier=1).then_inc(consts, 1)
            for n, (m, per, cnt) in enumerate(((head_of_row, HD, HH), (seq_of_row, RT, B))):
                pool.affine_select(out=m[:, :], in_=m[:, :], compare_op=ALU.is_ge, fill=0.0, base=0,
                                   pattern=[[-per, cnt]], channel_multiplier=1).then_inc(consts, 1)
                pool.wait_ge(consts, IDENTITIES + 1 + 2 * n)
                pool.affine_select(out=m[:, :], in_=m[:, :], compare_op=ALU.is_ge, fill=0.0, base=per - 1,
                                   pattern=[[per, cnt]], channel_multiplier=-1).then_inc(consts, 1)
            pad = xT[:, :, :].rearrange("p k (b t) -> p k b t", t=TP)[:, :, :, T:TP]
            pool.memset(pad, 0.0).then_inc(consts, 1)
            pool.wait_ge(l_pos, 16)
            pool.wait_ge(l_tokb, 16)
            pool.tensor_tensor(posb, posb, tokb[:, :].unsqueeze(1).to_broadcast([P, NPT, C]), ALU.add)\
                .then_inc(posb_done, 1)
            pool.memset(v[:, :, :, :], 1.0).then_inc(consts, 1)
            pool.wait_ge(l_mask, 16)
            pool.tensor_copy(mask[:, :], maskf).then_inc(mask_done, 1)
            pool.wait_ge(norm_a, NPT)
            pool.wait_ge(cls_x, 1)
            pool.wait_ge(l_wproj, 16 * 2)
            pool.memset(dif, NEG).then_inc(dif_init, 1)
            pool.tensor_tensor(h0[:, :, :], h0[:, :, :], bp[:, :].unsqueeze(1).to_broadcast([P, NT, C]),
                               ALU.add).then_inc(bproj_done, 1)
            pool.tensor_tensor(h0c[:, :], h0c[:, :], bp[0:B, :], ALU.add).then_inc(bproj_done, 1)

            def build_qblk(b, t, first=False):
                if not first:
                    pool.wait_ge(score_mm, b - 1)
                for f in range(2):
                    last = pool.tensor_tensor(
                        qblk[:, t, f, :, :, :],
                        qT[:, f, ds(b * TP, TP)].rearrange("p (i q) -> p i q", q=QB).unsqueeze(2)
                        .to_broadcast([P, NQ, HH, QB]),
                        head_of_row[:, :].unsqueeze(1).unsqueeze(3).to_broadcast([P, NQ, HH, QB]), ALU.mult)
                last.then_inc(qblk_done, 1)

            pool.wait_ge(patch_mm, NPT)
            pool.wait_ge(consts, V_ONES)
            pool.wait_ge(q_cp, 1)
            build_qblk(0, 0, first=True)
            build_qblk(1, 1, first=True)
            pool.wait_ge(q_cp, NG)
            with pool.Fori(1, B // 2) as i:
                for t in range(2):
                    build_qblk(i * 2 + t, t)

            y4 = yT[:, :, :].rearrange("p k (b t) -> p k b t", t=TP)

            def gather_ytile(j, slot):
                pool.tensor_copy(ytile[:, slot, :, :].rearrange("p k (b s) -> p k b s", s=RT),
                                 y4[:, :, :, ds(1 + j * RT, RT)]).then_inc(ytile_cp, 1)

            pool.wait_ge(yT_cp, B)
            gather_ytile(0, 0)
            gather_ytile(1, 1)
            with pool.Fori(1, NT // 2) as i:
                for t in range(2):
                    pool.wait_ge(proj_mm, i * 2 + t)
                    gather_ytile(i * 2 + t, t)
            pool.wait_ge(proj_mm, NT)
            gather_ytile(NT - 1, 0)

            pool.wait_ge(l_wall, 16)
            pool.wait_ge(r_dve, 11)

            def pick(b, t):
                e = pool.value_load(idx[0:1, ds(b, 1)], min_val=0, max_val=EXPERTS - 1)
                pool.tensor_copy(wsel[:, t:t + 1, :], wall[:, ds(e, 1), :]).then_inc(wsel_cp, 1)

            for t in range(G):
                pick(t, t)
            with pool.Fori(1, NG) as i:
                for t in range(G):
                    pool.wait_ge(up_mm, i * G + t - G + 1)
                    pick(i * G + t, t)

        @block.scalar
        def _(act):
            act.dma_start(wt[:, 0:KX // 2, :], wtok[:, 0:KX // 2, :]).then_inc(l_wt, 16)
            act.dma_start(h0c[:, :], cls_tok).then_inc(l_cls, 16)
            act.dma_start(xhc[:, :], pos_cls).then_inc(l_cls, 16)
            act.dma_start(colp[:, :, :], cols).then_inc(l_cols, 16)
            act.dma_start(wr[:, :, :], w_router).then_inc(l_cols, 16)
            act.dma_start(br[:, :], b_router).then_inc(l_cols, 16)
            act.dma_start(h0[:, NPT:NT, :], txt).then_inc(l_txt, 16)
            act.dma_start(maskf, causal).then_inc(l_mask, 16)
            act.dma_start(wlqv[:, :, :], w_lat_qv).then_inc(l_wattn, 16)
            act.dma_start(wlk[:, :, :], w_lat_k).then_inc(l_wattn, 16)
            act.dma_start(whq[:, :], w_heads_q).then_inc(l_wattn, 16)
            act.dma_start(whk[:, :], w_heads_k).then_inc(l_wattn, 16)
            act.dma_start(whv[LAT:P, :], w_heads_v).then_inc(l_wattn, 16)
            act.dma_start(wp[:, :, :], w_proj).then_inc(l_wproj, 16)
            act.dma_start(bp[:, :], b_proj).then_inc(l_wproj, 16)

            x4 = xT[:, :, :].rearrange("p k (b t) -> p k b t", t=TP)

            act.wait_ge(consts, FILLED)
            act.wait_ge(bn_dve, 1)
            act.activation(bn_tmp[:, :], bn_scale[:, :], ACT.Sqrt).then_inc(cls_sqrt, 1)
            act.wait_ge(cls_dve, 3)
            act.activation(sd[0:B, 0, 0:1], mv[0:B, 0, 0, 1:2], ACT.Sqrt, bias=eps_col[0:B, :]).then_inc(cls_sqrt, 1)
            act.wait_ge(xpose_a, 1)
            act.copy(x4[:, :, :, 0:1].rearrange("p k b o -> p k (b o)"),
                     ps[:, 6, 0:KC * B].rearrange("p (k b) -> p k b", k=KC)).then_inc(xT_done, 1)

            def evac_tiles(j, t, with_txt=True):
                act.wait_ge(xpose_a, j + 2)
                for u, at in ((0, 1), (1, 1 + NPATCH)):
                    if u and not with_txt:
                        continue
                    last = act.copy(
                        x4[:, :, :, j * RT + at:(j + 1) * RT + at],
                        ps[:, 3 + t, 2 * u * P:2 * (u + 1) * P].rearrange("p (k b s) -> p k b s", k=KC, s=RT))
                last.then_inc(xT_done, 1)

            def deviations(j, t):
                act.wait_ge(aggr_a, j + 1)
                nu = 2 if j < NTT else 1
                act.activation(sd[:, t, 0:nu], mv[:, t, 0:nu, 1], ACT.Sqrt, bias=eps_col[:, :]).then_inc(sqrt_a, 1)

            for j in range(NPT):
                deviations(j, j % 3)
                if j:
                    evac_tiles(j - 1, (j - 1) % 3)
            evac_tiles(NPT - 1, (NPT - 1) % 3, with_txt=False)

            def latqv_out(g, first=False):
                act.wait_ge(latqv_mm, g + 1)
                if not first:
                    act.wait_ge(q_mm, g)
                act.copy(latqv[:, :], ps[:, 0, 0:GN]).then_inc(latqv_cp, 1)

            def qv_out(g):
                act.wait_ge(v_mm, g * 2 + 2)
                act.copy(v[:, ds(g * G + 2, 2), :, 0:HD],
                         ps[0:TP, 7, :].rearrange("p (b h d) -> p b h d", b=2, h=HEADS)).then_inc(v_cpa, 1)
                act.wait_ge(q_mm, g + 1)
                act.activation(qT[:, :, ds(g * GN, GN)], ps[:, 2:4, 0:GN], ACT.Copy,
                               scale=float(HD) ** -0.5).then_inc(q_cp, 1)

            act.wait_ge(consts, V_ONES)
            latqv_out(0, first=True)
            with act.Fori(0, NG - 1) as i:
                act.wait_ge(v_mm, i * 2 + 2)
                act.copy(v[:, ds(i * G + 2, 2), :, 0:HD],
                         ps[0:TP, 7, :].rearrange("p (b h d) -> p b h d", b=2, h=HEADS)).then_inc(v_cpa, 1)
                latqv_out(i + 1)
                act.wait_ge(q_mm, i + 1)
                act.activation(qT[:, :, ds(i * GN, GN)], ps[:, 2:4, 0:GN], ACT.Copy,
                               scale=float(HD) ** -0.5).then_inc(q_cp, 1)
            qv_out(NG - 1)

            def yT_out(b):
                act.wait_ge(yT_xp, b + 1)
                act.copy(yT[:, :, ds(b * TP, TP)], ps[:, 7, 0:KC * TP].rearrange("p (k n) -> p k n", k=KC))\
                    .then_inc(yT_cp, 1)

            def exps(b, t, first=False):
                if not first:
                    act.wait_ge(pv_mm, b - 1)
                for k in range(3):
                    act.wait_ge(prob_xp, b * 3 + k + 1)
                    ni = min(2, NQ - 2 * k)
                    src = ps[0:TP, 2 + k, 0:ni * 2 * ROWS].rearrange("p (i h q) -> p i h q", i=ni, q=QB)
                    dst = prob[:, t, :, 2 * k * QB:(2 * k + ni) * QB].rearrange("p h (i q) -> p i h q", q=QB)
                    act.activation(dst, src, ACT.Exp).then_inc(exp_done, 1)

            exps(0, 0, first=True)
            exps(1, 1, first=True)
            with act.Fori(1, B // 2) as i:
                for t in range(2):
                    yT_out(i * 2 + t - 2)
                    exps(i * 2 + t, t)
            yT_out(B - 2)
            yT_out(B - 1)

            z4 = zT[:, :, :].rearrange("p k (b t) -> p k b t", t=TP)
            r4 = h1T[:, :, :].rearrange("p k (b t) -> p k b t", t=TP)

            def deviation_c(n, s, rows):
                act.wait_ge(aggr_c, n + 1)
                act.activation(sd[0:rows, s, 0:1], mv[0:rows, s, 0, 1:2], ACT.Sqrt, bias=eps2_col[0:rows, :],
                               scale=1.0 + EPS).then_inc(sqrt_c, 1)

            def evac_c(n, s, at, cnt):
                act.wait_ge(xpose_c, n + 1)
                for k in range(KC):
                    act.activation(z4[:, k, :, ds(at, cnt)],
                                   ps[:, 2 + s, k * B * cnt:(k + 1) * B * cnt].rearrange("p (b s) -> p b s", s=cnt),
                                   ACT.Identity, bias=colp[:, 1, k:k + 1], scale=colp[:, 0, k:k + 1])\
                        .then_inc(zT_cp, 1)
                src = ps[:, 6 + s, 0:KC * B * cnt].rearrange("p (k b s) -> p k b s", k=KC, s=cnt)
                if cnt == 1:
                    act.copy(r4[:, :, :, 0], src[:, :, :, 0]).then_inc(h1T_cp, 1)
                else:
                    act.copy(r4[:, :, :, ds(at, cnt)], src).then_inc(h1T_cp, 1)

            deviation_c(0, 0, B)
            deviation_c(1, 1, P)
            evac_c(0, 0, 0, 1)
            with act.Fori(0, (NT - 3) // 2) as i:
                for t in range(2):
                    deviation_c(i * 2 + t + 2, t, P)
                    evac_c(i * 2 + t + 1, 1 - t, (i * 2 + t) * RT + 1, RT)
            for n in range(NT - 1, NT + 1):
                deviation_c(n, n % 2, P)
                evac_c(n - 1, (n - 1) % 2, (n - 2) * RT + 1, RT)
            evac_c(NT, NT % 2, (NT - 1) * RT + 1, RT)

            act.wait_ge(r_dve, 4)
            act.activation(ex[:, :], lg[:, :], ACT.Exp, bias=ntop[:, :], accum_out=exs[:, :]).then_inc(r_act, 1)

            act.wait_ge(hid_ones, 1)

            def relu(b, t, first=False):
                act.wait_ge(down_mm, b + 1)
                if not first:
                    act.wait_ge(up_mm, b - G + 1)
                act.activation(hid[0:HID, t, :], ps[0:HID, t % 2, 0:T], ACT.Relu,
                               bias=wsel[0:HID, t, WPK - 1:WPK]).then_inc(relu_done, 1)

            for t in range(G):
                relu(t, t, first=True)
            with act.Fori(1, NG) as i:
                for t in range(G):
                    relu(i * G + t, t)

        @block.tensor
        def _(pe):
            pe.wait_ge(consts, IDENTITIES)
            pe.wait_ge(cls_x, 1)
            for k in range(KC):
                last = nc.tensor.transpose(ps[:, 6, k * B:(k + 1) * B], xhc[:, k * P:(k + 1) * P],
                                           ident[0:B, 0:B])
            last.then_inc(xpose_a, 1)

            def products(j, t, turn, first=False):
                pe.wait_ge(l_x[t], turn * 16 + 16)
                if not first:
                    pe.wait_ge(h_added, j - 2)
                for k in range(KX):
                    last = nc.tensor.matmul(ps[:, t, 0:C], xin[:, t, k, :], wt[:, k, :], start=(k == 0),
                                            stop=(k == KX - 1))
                last.then_inc(patch_mm, 1)

            def transposes(j, t, first=False, with_txt=True):
                pe.wait_ge(norm_a, j + 1)
                if not first:
                    pe.wait_ge(xT_done, j - 1)
                for u in range(2 if with_txt else 1):
                    for k in range(KC):
                        c = (2 * u + k) * P
                        last = nc.tensor.transpose(ps[:, 3 + t, c:c + P], xh[:, t, u, k * P:(k + 1) * P],
                                                   ident[:, :])
                last.then_inc(xpose_a, 1)

            pe.wait_ge(l_wt, 32)
            for j in range(NPT):
                products(j, j % 3, j // 3, first=(j < 3))
                if j:
                    transposes(j - 1, (j - 1) % 3, first=(j < 4))
            transposes(NPT - 1, (NPT - 1) % 3, with_txt=False)

            def latents(g, first=False):
                cols_ = ds(g * GN, GN)
                if not first:
                    pe.wait_ge(latqv_cp, g)
                for k in range(KC):
                    last = nc.tensor.matmul(ps[:, 0, 0:GN], wlqv[:, k, :], xT[:, k, cols_], start=(k == 0),
                                            stop=(k == KC - 1))
                last.then_inc(latqv_mm, 1)
                if not first:
                    pe.wait_ge(latk_cp, g)
                for k in range(KC):
                    last = nc.tensor.matmul(ps[:, 1, 0:GN], wlk[:, k, :], xT[:, k, cols_], start=(k == 0),
                                            stop=(k == KC - 1))
                last.then_inc(latk_mm, 1)

            def heads(g, first=False):
                pe.wait_ge(latqv_cp, g + 1)
                for u in range(2):
                    if not first:
                        pe.wait_ge((v_cpd, v_cpa)[u], g)
                    for w in range(2):
                        s = 2 * u + w
                        last = nc.tensor.matmul(ps[0:TP, 6 + u, w * C:(w + 1) * C],
                                                latqv[LAT:P, s * TP:(s + 1) * TP], whv[LAT:P, :],
                                                start=True, stop=True)
                    last.then_inc(v_mm, 1)
                if not first:
                    pe.wait_ge(q_cp, g)
                for k in range(KC):
                    last = nc.tensor.matmul(ps[:, 2 + k, 0:GN], whq[:, k * P:(k + 1) * P], latqv[0:LAT, :],
                                            start=True, stop=True)
                last.then_inc(q_mm, 1)
                pe.wait_ge(latk_cp, g + 1)
                if not first:
                    pe.wait_ge(k_cp, g)
                for k in range(KC):
                    last = nc.tensor.matmul(ps[:, 4 + k, 0:GN], whk[:, k * P:(k + 1) * P], latk[0:LAT, :],
                                            start=True, stop=True)
                last.then_inc(k_mm, 1)

            pe.wait_ge(l_wattn, 16 * 5)
            pe.wait_ge(xT_done, NPT + 1)
            pe.wait_ge(consts, PADDING)
            latents(0, first=True)
            latents(1)
            heads(0, first=True)
            with pe.Fori(1, NG - 1) as i:
                latents(i + 1)
                heads(i)
            heads(NG - 1)

            def scores(b, t, first=False):
                pe.wait_ge(qblk_done, b + 1)
                if not first:
                    pe.wait_ge(sub_done, b - 1)
                bank = ps[0:ROWS, t, :]
                nc.tensor.matmul(bank[:, 0:offset(NQ)], ident_bf[:, :], mask[:, :], start=True, stop=False,
                                 skip_group_check=True)
                for i in range(NQ):
                    for f in range(2):
                        c, w = offset(i) + f * width(i), width(i)
                        last = nc.tensor.matmul(bank[:, c:c + w], qblk[:, t, f, i, :, :].rearrange("p h q -> p (h q)"),
                                                kT[:, f, ds(b * TP, w)], start=False,
                                                stop=(i == NQ - 1 and f == 1), skip_group_check=True)
                last.then_inc(score_mm, 1)

            def prob_transposes(b, t, first=False):
                pe.wait_ge(sub_done, b + 1)
                for k in range(3):
                    if not first:
                        pe.wait_ge(exp_done, b * 3 - 2 + k)
                    for n, i in enumerate(range(2 * k, min(2 * k + 2, NQ))):
                        for f in range(2):
                            c = (2 * n + f) * ROWS
                            last = nc.tensor.transpose(ps[0:TP, 2 + k, c:c + ROWS], dif[:, t, f, i, :],
                                                       ident[0:ROWS, 0:ROWS])
                    last.then_inc(prob_xp, 1)

            def weighted_values(b, t, first=False):
                pe.wait_ge(exp_done, b * 3 + 3)
                if not first:
                    pe.wait_ge(ynorm, b - 1)
                for h in range(HEADS):
                    last = nc.tensor.matmul(ps[0:TP, 5 + t, h * VW:(h + 1) * VW], prob[:, t, h, :],
                                            v[:, ds(b, 1), h, :].rearrange("p o d -> p (o d)"),
                                            start=True, stop=True)
                last.then_inc(pv_mm, 1)

            def y_transposes(b, t, first=False):
                pe.wait_ge(ynorm, b + 1)
                if not first:
                    pe.wait_ge(yT_cp, b)
                for k in range(KC):
                    last = nc.tensor.transpose(ps[:, 7, k * TP:(k + 1) * TP], yn[:, t, k * P:(k + 1) * P],
                                               ident[0:TP, 0:TP])
                last.then_inc(yT_xp, 1)

            pe.wait_ge(mask_done, 1)
            pe.wait_ge(latqv_cp, NG)
            pe.wait_ge(latk_cp, NG)
            pe.wait_ge(k_cp, NG)
            scores(0, 0, first=True)
            scores(1, 1, first=True)
            pe.wait_ge(q_cp, NG)
            pe.wait_ge(v_cpa, NG)
            pe.wait_ge(v_cpd, NG)
            prob_transposes(0, 0, first=True)
            scores(2, 0)
            prob_transposes(1, 1)
            weighted_values(0, 0, first=True)

            def attend(b, t, end=False):
                if not end:
                    scores(b + 1, 1 - t)
                y_transposes(b - 2, t, first=isinstance(b, int) and b == 2)
                prob_transposes(b, t)
                weighted_values(b - 1, 1 - t, first=isinstance(b, int) and b == 2)

            for b in range(2, 4):
                attend(b, b % 2)
            with pe.Fori(2, B // 2 - 1) as i:
                for t in range(2):
                    attend(i * 2 + t, t)
            for b in range(B - 2, B):
                attend(b, b % 2, end=(b + 1 == B))
            y_transposes(B - 2, 0)
            weighted_values(B - 1, 1)
            y_transposes(B - 1, 1)

            y4 = yT[:, :, :].rearrange("p k (b t) -> p k b t", t=TP)

            def project(n, s, cls=False):
                rows = B if cls else P
                if not cls:
                    pe.wait_ge(ytile_cp, n)
                for k in range(KC):
                    lhsT = y4[:, k, :, 0] if cls else ytile[:, 1 - s, k, :]
                    last = nc.tensor.matmul(ps[0:rows, s, 0:C], lhsT, wp[:, k, :], start=(k == 0),
                                            stop=(k == KC - 1))
                last.then_inc(proj_mm, 1)

            def ln2_out(n, s, cls=False, end=False):
                rows = B if cls else P
                pe.wait_ge(zh_done, n + 1)
                for k in range(KC):
                    nc.tensor.transpose(ps[:, 2 + s, k * rows:(k + 1) * rows], zh[0:rows, s, k * P:(k + 1) * P],
                                        ident[0:rows, 0:rows])
                for k in range(KC):
                    nc.tensor.transpose(ps[:, 6 + s, k * rows:(k + 1) * rows], h1[0:rows, s, k * P:(k + 1) * P],
                                        ident[0:rows, 0:rows])
                for k in range(KC):
                    last = nc.tensor.matmul(ps[:, 4 + k, 0:B], zh[0:rows, s, k * P:(k + 1) * P],
                                            ident[0:B, 0:B] if cls else seq_of_row[:, :], start=cls, stop=end,
                                            skip_group_check=True)
                last.then_inc(xpose_c, 1)

            pe.wait_ge(yT_cp, B)
            pe.wait_ge(l_wproj, 32)
            project(0, 0, cls=True)
            project(1, 1)
            ln2_out(0, 0, cls=True)

            def out_step(n, s, first=False):
                pe.wait_ge(h1_done, n - 1)
                project(n, s)
                if not first:
                    pe.wait_ge(h1T_cp, n - 2)
                ln2_out(n - 1, 1 - s)

            for n in range(2, 4):
                out_step(n, n % 2, first=(n == 2))
            with pe.Fori(1, (NT - 3) // 2) as i:
                for t in range(2):
                    out_step(i * 2 + t + 2, t)
            for n in range(NT - 1, NT + 1):
                out_step(n, n % 2)
            pe.wait_ge(h1T_cp, NT - 1)
            ln2_out(NT, NT % 2, end=True)

            pe.wait_ge(r_dve, 1)
            for k in range(KC):
                last = nc.tensor.matmul(ps[0:B, 0, 0:EXPERTS], zbn[:, k, :], wr[:, k, :], start=(k == 0),
                                        stop=(k == KC - 1))
            last.then_inc(r_logit, 1)
            pe.wait_ge(r_dve, 10)
            nc.tensor.matmul(ps[:, 4, 0:B], gate_col[:, :], ident[0:B, 0:B], start=True, stop=True)
            nc.tensor.matmul(ps[0:1, 5, 0:B], idx_col[:, :], ident[0:B, 0:B], start=True, stop=True)\
                .then_inc(r_bcast, 1)

            def down(b, t):
                for k in range(KC):
                    last = nc.tensor.matmul(ps[0:HID, t % 2, 0:T], wsel[:, t, k * HID:(k + 1) * HID],
                                            zT[:, k, ds(b * TP, T)], start=(k == 0), stop=(k == KC - 1))
                last.then_inc(down_mm, 1)

            def up(b, t):
                for k in range(KC):
                    c = KC * HID + k * P
                    last = nc.tensor.matmul(ps[:, 2 + t % 2, k * T:(k + 1) * T], wsel[0:HID + 1, t, c:c + P],
                                            hid[:, t, :], start=True, stop=True)
                last.then_inc(up_mm, 1)

            def ffn_step(b, t, first=False, end=False):
                if not end:
                    pe.wait_ge(wsel_cp, b + 3)
                if not first:
                    pe.wait_ge(out_done, b - 1)
                pe.wait_ge(relu_done, b + 1)
                up(b, t)
                if not end:
                    down(b + 2, (t + 2) % G)

            pe.wait_ge(h1T_cp, NT + 1)
            for b in range(2):
                pe.wait_ge(wsel_cp, b + 1)
                down(b, b)
            for b in range(G):
                ffn_step(b, b, first=(b < 2))
            with pe.Fori(1, NG - 1) as i:
                for t in range(G):
                    ffn_step(i * G + t, t)
            for b in range(B - G, B):
                ffn_step(b, b % G, end=(b + 2 >= B))

        @block.vector
        def _(dve):
            nc.vector.memset(hid[HID:HID + 1, :, :], 1.0).then_inc(hid_ones, 1)
            dve.wait_ge(l_cols, 48)
            nc.vector.tensor_scalar(bn_scale[:, :], colp[:, 5, :], EPS, None, ALU.add).then_inc(bn_dve, 1)
            dve.wait_ge(cls_sqrt, 1)
            nc.vector.reciprocal(bn_scale[:, :], bn_tmp[:, :]).then_inc(bn_dve, 1)
            dve.wait_ge(bn_dve, 2)
            nc.vector.tensor_tensor(bn_scale[:, :], bn_scale[:, :], colp[:, 2, :], ALU.mult).then_inc(bn_dve, 1)
            nc.vector.tensor_tensor(zs_shift[:, :], colp[:, 1, :], colp[:, 4, :], ALU.subtract).then_inc(bn_dve, 1)
            dve.wait_ge(bn_dve, 4)
            nc.vector.scalar_tensor_tensor(zs_scale[:, :], bn_scale[:, :], 1.0 / T, colp[:, 0, :], ALU.mult,
                                           ALU.mult).then_inc(bn_dve, 1)
            nc.vector.tensor_tensor(bn_tmp[:, :], zs_shift[:, :], bn_scale[:, :], ALU.mult).then_inc(bn_dve, 1)
            dve.wait_ge(bn_dve, 6)
            nc.vector.tensor_tensor(zs_shift[:, :], bn_tmp[:, :], colp[:, 3, :], ALU.add).then_inc(bn_dve, 1)

            dve.wait_ge(l_cls, 32)
            nc.vector.tensor_tensor(h0c[:, :], h0c[:, :], xhc[:, :], ALU.add).then_inc(cls_dve, 1)
            dve.wait_ge(cls_dve, 1)
            nc.vector.bn_stats(st[0:B, 0, 0, :], h0c[:, :]).then_inc(cls_dve, 1)
            dve.wait_ge(cls_dve, 2)
            nc.vector.bn_aggr(mv[0:B, 0, 0, :], st[0:B, 0, 0, :]).then_inc(cls_dve, 1)
            dve.wait_ge(cls_sqrt, 2)
            nc.vector.reciprocal(rs[0:B, 0, 0:1], sd[0:B, 0, 0:1]).then_inc(cls_dve, 1)
            dve.wait_ge(cls_dve, 4)
            nc.vector.tensor_scalar(xhc[:, :], h0c[:, :], mv[0:B, 0, 0, 0:1], rs[0:B, 0, 0:1], ALU.subtract,
                                    ALU.mult).then_inc(cls_x, 1)

            def ln1(j, t, first=False, with_txt=True):
                nu = 2 if with_txt else 1
                if with_txt:
                    nc.vector.bn_stats(st[:, t, 1, :], h0[:, j + NPT, :])
                dve.wait_ge(patch_mm, j + 1)
                nc.vector.tensor_tensor(h0[:, j, :], ps[:, t, 0:C], posb[:, j, :], ALU.add).then_inc(h_added, 1)
                dve.wait_ge(h_added, j + 1)
                nc.vector.bn_stats(st[:, t, 0, :], h0[:, j, :]).then_inc(stats_a, 1)
                dve.wait_ge(stats_a, j + 1)
                for u in range(nu):
                    last = nc.vector.bn_aggr(mv[:, t, u, :], st[:, t, u, :])
                last.then_inc(aggr_a, 1)
                dve.wait_ge(sqrt_a, j + 1)
                nc.vector.reciprocal(rs[:, t, 0:nu], sd[:, t, 0:nu]).then_inc(recip_a, 1)
                dve.wait_ge(recip_a, j + 1)
                if not first:
                    dve.wait_ge(xpose_a, j - 1)
                for u in range(nu):
                    last = nc.vector.tensor_scalar(xh[:, t, u, :], h0[:, j + u * NPT, :], mv[:, t, u, 0:1], rs[:, t, u:u + 1],
                                                   ALU.subtract, ALU.mult)
                last.then_inc(norm_a, 1)

            dve.wait_ge(cls_x, 1)
            dve.wait_ge(l_txt, 16)
            dve.wait_ge(posb_done, 1)
            for j in range(NPT):
                ln1(j, j % 3, first=(j < 3), with_txt=(j < NTT))

            def latk_out(g, first=False):
                dve.wait_ge(latk_mm, g + 1)
                if not first:
                    dve.wait_ge(k_mm, g)
                nc.vector.tensor_copy(latk[0:LAT, :], ps[0:LAT, 1, 0:GN]).then_inc(latk_cp, 1)

            def kv_out(g):
                dve.wait_ge(v_mm, g * 2 + 1)
                nc.vector.tensor_copy(v[:, ds(g * G, 2), :, 0:HD],
                                      ps[0:TP, 6, :].rearrange("p (b h d) -> p b h d", b=2, h=HEADS))\
                    .then_inc(v_cpd, 1)
                dve.wait_ge(k_mm, g + 1)
                nc.vector.tensor_copy(kT[:, :, ds(g * GN, GN)], ps[:, 4:6, 0:GN]).then_inc(k_cp, 1)

            dve.wait_ge(consts, V_ONES)
            latk_out(0, first=True)
            with dve.Fori(0, NG - 1) as i:
                kv_out(i)
                latk_out(i + 1)
            kv_out(NG - 1)

            def shift(b, t, first=False):
                dve.wait_ge(score_mm, b + 1)

                def block(i):
                    return ps[0:ROWS, t, offset(i):offset(i + 1)].rearrange("p (f w) -> p f w", f=2)

                for i in range(NQ):
                    last = nc.vector.tensor_reduce(mx[:, t, i, :], block(i), AX_X, ALU.max)
                last.then_inc(max_done, 1)
                dve.wait_ge(max_done, b + 1)
                if not first:
                    dve.wait_ge(prob_xp, b * 3 - 3)
                for i in range(NQ):
                    w = width(i)
                    last = nc.vector.tensor_tensor(dif[:, t, :, i, 0:w], block(i),
                                                   mx[:, t, i, :].unsqueeze(2).to_broadcast([ROWS, 2, w]),
                                                   ALU.subtract)
                last.then_inc(sub_done, 1)

            def normalise(b, t, first=False):
                dve.wait_ge(pv_mm, b + 1)
                o = ps[0:TP, 5 + t, 0:HEADS * VW].rearrange("p (h d) -> p h d", d=VW)
                nc.vector.reciprocal(rc[:, t, :], o[:, :, HD]).then_inc(rec_done, 1)
                dve.wait_ge(rec_done, b + 1)
                if not first:
                    dve.wait_ge(yT_xp, b - 1)
                nc.vector.tensor_tensor(yn[:, t, :].rearrange("p (h d) -> p h d", d=HD), o[:, :, 0:HD],
                                        rc[:, t, :].unsqueeze(2).to_broadcast([TP, HEADS, HD]), ALU.mult)\
                    .then_inc(ynorm, 1)

            dve.wait_ge(dif_init, 1)
            shift(0, 0, first=True)
            shift(1, 1, first=True)
            shift(2, 0)
            normalise(0, 0, first=True)
            shift(3, 1)
            normalise(1, 1, first=True)
            with dve.Fori(1, B // 2 - 1) as i:
                for t in range(2):
                    b = i * 2 + t
                    shift(b + 2, t)
                    normalise(b, t)
            normalise(B - 2, 0)
            normalise(B - 1, 1)

            def add_residual(n, s, j, cls=False):
                rows = B if cls else P
                old = h0c[:, :] if cls else h0[:, ds(j, 1), :].rearrange("p o n -> p (o n)")
                dve.wait_ge(proj_mm, n + 1)
                nc.vector.tensor_tensor(h1[0:rows, s, :], ps[0:rows, s, 0:C], old, ALU.add).then_inc(h1_done, 1)

            def take_stats(n, s, rows=P):
                dve.wait_ge(h1_done, n + 1)
                nc.vector.bn_stats(st[0:rows, s, 0, :], h1[0:rows, s, :]).then_inc(stats_c, 1)

            def merge_stats(s, rows=P):
                nc.vector.bn_aggr(mv[0:rows, s, 0, :], st[0:rows, s, 0, :]).then_inc(aggr_c, 1)

            def invert(n, s, rows=P):
                dve.wait_ge(sqrt_c, n + 1)
                nc.vector.reciprocal(rs[0:rows, s, 0:1], sd[0:rows, s, 0:1]).then_inc(recip_c, 1)

            def standardise(n, s, rows=P):
                dve.wait_ge(recip_c, n + 1)
                nc.vector.tensor_scalar(zh[0:rows, s, :], h1[0:rows, s, :], mv[0:rows, s, 0, 0:1],
                                        rs[0:rows, s, 0:1], ALU.subtract, ALU.mult).then_inc(zh_done, 1)

            def ln2_step(n, s, before=P):
                add_residual(n, s, n - 1)
                invert(n - 1, 1 - s, before)
                take_stats(n, s)
                dve.wait_ge(stats_c, n + 1)
                standardise(n - 1, 1 - s, before)
                merge_stats(s)

            dve.wait_ge(bproj_done, 2)
            add_residual(0, 0, 0, cls=True)
            take_stats(0, 0, B)
            dve.wait_ge(stats_c, 1)
            merge_stats(0, B)
            ln2_step(1, 1, before=B)
            with dve.Fori(0, (NT - 3) // 2) as i:
                for t in range(2):
                    n = i * 2 + t + 2
                    dve.wait_ge(xpose_c, n - 1)
                    ln2_step(n, t)
            for n in range(NT - 1, NT + 1):
                dve.wait_ge(xpose_c, n - 1)
                ln2_step(n, n % 2)
            invert(NT, NT % 2)
            standardise(NT, NT % 2)

            dve.wait_ge(xpose_c, NT + 1)
            for k in range(KC):
                last = nc.vector.tensor_scalar(zbn[:, k, :], ps[:, 4 + k, 0:B], zs_scale[:, k:k + 1],
                                               zs_shift[:, k:k + 1], ALU.mult, ALU.add)
            last.then_inc(r_dve, 1)
            dve.wait_ge(r_logit, 1)
            nc.vector.tensor_tensor(lg[:, :], ps[0:B, 0, 0:EXPERTS], br[:, :], ALU.add).then_inc(r_dve, 1)
            dve.wait_ge(r_dve, 2)
            nc.vector.max(top[:, :], lg[:, :]).then_inc(r_dve, 1)
            dve.wait_ge(r_dve, 3)
            nc.vector.tensor_scalar(ntop[:, :], top[:, 0:1], -1.0, None, ALU.mult).then_inc(r_dve, 1)
            dve.wait_ge(r_act, 1)
            nc.vector.reciprocal(exr[:, :], exs[:, :]).then_inc(r_dve, 1)
            dve.wait_ge(r_dve, 5)
            nc.vector.tensor_scalar(pr[:, :], ex[:, :], exr[:, 0:1], None, ALU.mult).then_inc(r_dve, 1)
            dve.wait_ge(r_dve, 6)
            nc.vector.max(ptop[:, :], pr[:, :]).then_inc(r_dve, 1)
            dve.wait_ge(r_dve, 7)
            nc.vector.max_index(pidx[:, :], ptop[:, :], pr[:, :]).then_inc(r_dve, 1)
            dve.wait_ge(r_dve, 8)
            nc.vector.tensor_copy(idx_col[:, :], pidx[:, 0:1]).then_inc(r_dve, 1)
            nc.vector.tensor_copy(gate_col[:, :], ptop[:, 0:1].to_broadcast([B, P])).then_inc(r_dve, 1)
            dve.wait_ge(r_bcast, 1)
            nc.vector.tensor_copy(idx[:, :], ps[0:1, 5, 0:B]).then_inc(r_dve, 1)
            nc.vector.tensor_copy(gate[:, :], ps[:, 4, 0:B]).then_inc(r_dve, 1)

            def finish(b, g, t):
                dve.wait_ge(up_mm, b + 1)
                nc.vector.scalar_tensor_tensor(
                    oT[:, ds(g, 1), :, t * T:(t + 1) * T].rearrange("p o k n -> p (o k) n"),
                    ps[:, 2 + t % 2, 0:KC * T].rearrange("p (k n) -> p k n", k=KC), gate[:, ds(b, 1)],
                    h1T[:, :, ds(b * TP, T)], ALU.mult, ALU.add).then_inc(out_done, 1)

            dve.wait_ge(h1T_cp, NT + 1)
            dve.wait_ge(r_dve, 12)
            with dve.Fori(0, NG) as i:
                for t in range(G):
                    finish(i * G + t, i, t)


_OUT = (NG, P, KC * G * T)


def kernel(**inputs):
    import concourse.bacc as bacc
    from concourse.bass_utils import run_bass_kernel_spmd as run

    a = {k: np.asarray(v) for k, v in inputs.items()}
    con = np.ascontiguousarray

    x = a["x"].reshape(B, 3, 6, 16, 6, 16).transpose(0, 2, 4, 1, 3, 5).reshape(B, NPT, RT, KX, P)
    patches = x.transpose(1, 4, 3, 0, 2).reshape(NPT, P, KX, P)
    tiled = lambda w: w.reshape(-1, P, w.shape[-1]).transpose(1, 0, 2)
    pos = a["L0_tok_pos_embedding"][0]
    pos_rows = np.broadcast_to(pos[1:1 + NPATCH].reshape(NPT, RT, C).transpose(1, 0, 2), (B, RT, NPT, C))
    rows = lambda r, n: np.broadcast_to(r.reshape(1, -1), (n, r.size))
    col = lambda r: r.reshape(KC, P).T
    up_ = np.zeros((EXPERTS, P, C), np.float32)
    up_[:, 0:HID] = a["L0_ffn_W_up"]
    up_[:, HID] = a["L0_ffn_b_up"]
    bd = np.zeros((EXPERTS, P, 1), np.float32)
    bd[:, 0:HID, 0] = a["L0_ffn_b_down"]
    down_ = a["L0_ffn_W_down"].reshape(EXPERTS, KC, P, HID).transpose(0, 2, 1, 3).reshape(EXPERTS, P, KC * HID)
    causal = np.zeros((HH, QB, offset(NQ)), np.float32)
    for i in range(NQ):
        late = np.arange(width(i))[None, :] > i * QB + np.arange(QB)[:, None]
        causal[:, :, offset(i):offset(i + 1)] = np.tile(np.where(late, np.float32(NEG), np.float32(0)), (1, 2))
    arrays = dict(
        patches=patches, wtok=tiled(a["L0_tok_W"].T),
        txt=a["txt"].reshape(B, NTT, RT, C).transpose(0, 2, 1, 3).reshape(P, NTT, C),
        pos_rows=pos_rows.reshape(P, NPT, C), tok_b=rows(a["L0_tok_b"], P),
        cls_tok=rows(a["L0_tok_class_token"], B), pos_cls=rows(pos[0], B),
        w_lat_qv=tiled(np.concatenate([a["L0_attn_wq_lat"], a["L0_attn_wv_lat"]], 1)),
        w_lat_k=tiled(np.concatenate([a["L0_attn_wk_lat"]] * 2, 1)), w_heads_q=a["L0_attn_wq_heads"], w_heads_k=a["L0_attn_wk_heads"],
        w_heads_v=a["L0_attn_wv_heads"], w_proj=tiled(a["L0_attn_w_proj"]), b_proj=rows(a["L0_attn_b_proj"], P),
        cols=np.stack([col(a["L0_ffn_" + n]) for n in ("ln_g", "ln_b", "bn_g", "bn_b", "bn_mean", "bn_var")], 1),
        w_router=tiled(a["L0_ffn_Wr"]), b_router=rows(a["L0_ffn_br"], B),
        experts=np.concatenate([down_, up_, bd], 2).transpose(1, 0, 2),
        causal=causal.reshape(ROWS, offset(NQ)))

    nc = bacc.Bacc("TRN2", target_bir_lowering=False, num_devices=1)
    arrays = {f"in_{k}": con(v) for k, v in arrays.items()}
    args = [nc.dram_tensor(k, v.shape, F32, kind="ExternalInput").ap() for k, v in arrays.items()]
    out = nc.dram_tensor("out_rows", _OUT, F32, kind="ExternalOutput").ap()
    early_fusion(nc, *args, out)
    r = run(nc, [arrays], core_ids=[0])
    got = np.asarray(r.results[0]["out_rows"])
    got = got.reshape(NG, P, KC, G, T).transpose(0, 3, 4, 2, 1)
    return con(got.reshape(B, T, C))
```

```python
from contextlib import ExitStack

import numpy as np

import concourse.bass as bass
from concourse import mybir

ALU = mybir.AluOpType
ACT = mybir.ActivationFunctionType
F32 = mybir.dt.float32
BF16 = mybir.dt.bfloat16
I32 = mybir.dt.int32
U32 = mybir.dt.uint32
AX_X = mybir.AxisListType.X
ds = bass.ds

P = 128
B = 32
NPATCH, NTXT = 36, 32
T = 1 + NPATCH + NTXT
TP = T + 1
C = 256
KC = C // P
KX = 3 * 16 * 16 // P
RT = 4
NPT, NTT = NPATCH // RT, NTXT // RT
NT = NPT + NTT
assert (NT + 1) % 3 == 0
HEADS, HD, LAT = 16, 16, 64
HH = P // HD
HQ = 4
HC = HQ * TP
VS = P // HQ
G = 4
GN = G * TP
NG = B // G
EXPERTS, HID = 8, 64
EPS = 1e-5
NEG = -1e30
WDN = KC * HID + 1
WPK = WDN + C


def early_fusion(nc, patches, wtok, txt, pos_rows, tok_b, cls_tok, pos_cls, w_lat_qv, w_lat_k, w_heads_q,
                 w_heads_k, w_heads_v, w_proj, b_proj, cols, w_router, b_router, experts, out):
    with ExitStack() as ctx:
        def sb(name, shape, dt=F32):
            return ctx.enter_context(nc.sbuf_tensor(name, shape, dt))

        def sem(name):
            return ctx.enter_context(nc.semaphore(name))

        ident = sb("ident", [P, P])
        ident_bf = sb("ident_bf", [TP, TP], BF16)
        mask = sb("mask", [TP, HQ, TP], BF16)
        head_of_row = sb("head_of_row", [P, HH])
        seq_of_row = sb("seq_of_row", [P, B])
        h0 = sb("h0", [P, NT, C])
        h0c = sb("h0c", [B, C])
        xT = sb("xT", [P, KC, B * TP])
        qT = sb("qT", [P, KC, B * TP])
        kT = sb("kT", [P, KC, B * TP])
        yT = sb("yT", [P, KC, B * TP])
        v = sb("v", [TP, B, C])
        zT, h1T = xT, qT
        oT = kT[:, :, :].rearrange("p k n -> p (k n)")[:, 0:NG * KC * G * T]\
            .rearrange("p (g k n) -> p g k n", g=NG, k=KC)
        wlqv = sb("wlqv", [P, KC, P])
        wlk = sb("wlk", [P, KC, P])
        whq = sb("whq", [LAT, C])
        whk = sb("whk", [LAT, C])
        whv = sb("whv", [P, C])
        latqv = sb("latqv", [P, GN])
        latk = sb("latk", [P, GN])
        wp = sb("wp", [P, KC, C])
        bp = sb("bp", [P, C])
        tokb = sb("tokb", [P, C])
        colp = sb("colp", [P, 6, KC])
        eps_col = sb("eps_col", [P, 1])
        eps2_col = sb("eps2_col", [P, 1])
        bn_scale = sb("bn_scale", [P, KC])
        bn_tmp = sb("bn_tmp", [P, KC])
        zs_scale = sb("zs_scale", [P, KC])
        zs_shift = sb("zs_shift", [P, KC])
        wr = sb("wr", [P, KC, EXPERTS])
        br = sb("br", [B, EXPERTS])
        wall = sb("wall", [P, EXPERTS, WPK])
        wsel = sb("wsel", [P, G, WPK])
        hid = sb("hid", [HID + 1, G, T])
        xh = sb("xh", [P, 3, 2, C])
        xhc = sb("xhc", [B, C])
        st = sb("st", [P, 3, 2, 6])
        mv = sb("mv", [P, 3, 2, 2])
        sd = sb("sd", [P, 3, 2])
        rs = sb("rs", [P, 3, 2])
        ytile = sb("ytile", [P, 3, KC, P])
        h1 = sb("h1", [P, 3, C])
        zh = sb("zh", [P, 3, C])
        area = sb("area", [P, KX * C + 3 * KX * P + NPT * C])
        wt = area[:, 0:KX * C].rearrange("p (k n) -> p k n", k=KX)
        xin = area[:, KX * C:KX * C + 3 * KX * P].rearrange("p (s k n) -> p s k n", s=3, k=KX)
        posb = area[:, KX * C + 3 * KX * P:].rearrange("p (j n) -> p j n", j=NPT)
        at = 0

        def piece(rows, dims):
            nonlocal at
            n = int(np.prod(dims))
            flat = area[0:rows, at:at + n]
            at += n
            names = " ".join("abcd"[:len(dims)])
            return flat.rearrange(f"p ({names}) -> p {names}", **dict(zip("abcd", dims)))

        kblk = piece(P, (KC, 2, HQ, TP))
        dif = piece(TP, (KC, 2, HQ, TP))
        prob = piece(TP, (KC, 2, HQ, TP))
        qs = piece(P, (2, KC, TP))
        vs = piece(TP, (2, HEADS, VS))
        yraw = piece(P, (KC, 2, TP))
        mx = sb("mx", [TP, KC, 2, HQ])
        rc = sb("rc", [TP, HEADS])
        yn = sb("yn", [TP, C])
        zbn = sb("zbn", [P, KC, B])
        lg = sb("lg", [B, EXPERTS])
        top = sb("top", [B, 8])
        ntop = sb("ntop", [B, 1])
        ex = sb("ex", [B, EXPERTS])
        exs = sb("exs", [B, 1])
        exr = sb("exr", [B, 1])
        pr = sb("pr", [B, EXPERTS])
        ptop = sb("ptop", [B, 8])
        pidx = sb("pidx", [B, 8], U32)
        gate_col = sb("gate_col", [B, P])
        idx_col = sb("idx_col", [B, 1])
        gate = sb("gate", [P, B])
        idx = sb("idx", [1, B], I32)
        ps = ctx.enter_context(nc.psum_tensor("ps", [P, 8, 512], F32))

        l_txt, l_pos, l_pos_rest, l_tokb, l_cls = (sem(n) for n in
                                                   ("l_txt", "l_pos", "l_pos_rest", "l_tokb", "l_cls"))
        l_wt = [sem(f"l_wt{h}") for h in range(2)]
        l_x = [sem(f"l_x{t}") for t in range(3)]
        l_wattn, l_wproj, l_cols, l_wall = (sem(n) for n in ("l_wattn", "l_wproj", "l_cols", "l_wall"))
        consts, posb_done, bproj_done = sem("consts"), sem("posb_done"), sem("bproj_done")
        mask_done, vs_ones, hid_ones = sem("mask_done"), sem("vs_ones"), sem("hid_ones")
        patch_mm, h_added, stats_a, aggr_a, sqrt_a, recip_a, norm_a, xpose_a, xT_done = (
            sem(n) for n in ("patch_mm", "h_added", "stats_a", "aggr_a", "sqrt_a", "recip_a", "norm_a",
                             "xpose_a", "xT_done"))
        cls_dve, cls_sqrt, cls_x, bn_dve = sem("cls_dve"), sem("cls_sqrt"), sem("cls_x"), sem("bn_dve")
        latqv_mm, latk_mm, latqv_cp, latk_cp, v_mm, q_mm, k_mm, q_cp, k_cp, v_cpa, v_cpd = (
            sem(n) for n in ("latqv_mm", "latk_mm", "latqv_cp", "latk_cp", "v_mm", "q_mm", "k_mm", "q_cp",
                             "k_cp", "v_cpa", "v_cpd"))
        qs_done, kblk_done, vs_done, score_mm, max_done, sub_done, prob_xp, exp_done = (
            sem(n) for n in ("qs_done", "kblk_done", "vs_done", "score_mm", "max_done", "sub_done",
                             "prob_xp", "exp_done"))
        pv_mm, yraw_cp, yraw_xp, rec_done, ynorm, yT_xp, yT_cp = (
            sem(n) for n in ("pv_mm", "yraw_cp", "yraw_xp", "rec_done", "ynorm", "yT_xp", "yT_cp"))
        ytile_cp, proj_mm, h1_done, stats_c, aggr_c, sqrt_c, recip_c, zh_done, xpose_c, zT_cp, h1T_cp = (
            sem(n) for n in ("ytile_cp", "proj_mm", "h1_done", "stats_c", "aggr_c", "sqrt_c", "recip_c",
                             "zh_done", "xpose_c", "zT_cp", "h1T_cp"))
        r_dve, r_act, r_logit, r_bcast = sem("r_dve"), sem("r_act"), sem("r_logit"), sem("r_bcast")
        wdown_cp, wup_cp, down_mm, relu_done, up_mm, out_done, stored = (
            sem(n) for n in ("wdown_cp", "wup_cp", "down_mm", "relu_done", "up_mm", "out_done", "stored"))

        FILLED, IDENTITIES, PADDING = 6, 8, 13

        PROJ, XP = (0, 1, 7), (2, 3, 6)

        block = ctx.enter_context(nc.Block())

        @block.sync
        def _(sp):
            def load_patch(j, t):
                sp.dma_start(xin[:, t, :, :], patches[j, :, :, :]).then_inc(l_x[t], 16)

            load_patch(0, 0)
            sp.dma_start(wt[:, KX // 2:KX, :], wtok[:, KX // 2:KX, :]).then_inc(l_wt[1], 16)
            load_patch(1, 1)
            sp.dma_start(posb[:, 0:3, :], pos_rows[:, 0:3, :]).then_inc(l_pos, 16)
            load_patch(2, 2)
            sp.dma_start(posb[:, 3:NPT, :], pos_rows[:, 3:NPT, :]).then_inc(l_pos_rest, 16)
            for j in range(3, NPT):
                sp.wait_ge(patch_mm, j - 2)
                load_patch(j, j % 3)
            sp.dma_start(wall[:, :, :], experts).then_inc(l_wall, 16)
            with sp.Fori(0, NG) as i:
                sp.wait_ge(out_done, i * G + G)
                sp.dma_start(out[ds(i, 1), :, :].rearrange("o p n -> (o p) n"),
                             oT[:, ds(i, 1), :, :].rearrange("p o k n -> p (o k n)")).then_inc(stored, 16)
            sp.wait_ge(stored, 16 * NG)

        @block.gpsimd
        def _(pool):
            pool.memset(ident[:, :], 0.0).then_inc(consts, 1)
            pool.memset(ident_bf[:, :], 0.0).then_inc(consts, 1)
            pool.memset(head_of_row[:, :], 1.0).then_inc(consts, 1)
            pool.memset(seq_of_row[:, :], 1.0).then_inc(consts, 1)
            pool.memset(eps_col[:, :], EPS).then_inc(consts, 1)
            pool.memset(eps2_col[:, :], EPS * EPS).then_inc(consts, 1)
            pool.wait_ge(consts, FILLED)
            for m, n in ((ident, P), (ident_bf, TP)):
                pool.affine_select(out=m[:, :], in_=m[:, :], compare_op=ALU.not_equal, fill=1.0, base=0,
                                   pattern=[[-1, n]], channel_multiplier=1).then_inc(consts, 1)
            for n, (m, per, cnt) in enumerate(((head_of_row, HD, HH), (seq_of_row, RT, B))):
                pool.affine_select(out=m[:, :], in_=m[:, :], compare_op=ALU.is_ge, fill=0.0, base=0,
                                   pattern=[[-per, cnt]], channel_multiplier=1).then_inc(consts, 1)
                pool.wait_ge(consts, IDENTITIES + 1 + 2 * n)
                pool.affine_select(out=m[:, :], in_=m[:, :], compare_op=ALU.is_ge, fill=0.0, base=per - 1,
                                   pattern=[[per, cnt]], channel_multiplier=-1).then_inc(consts, 1)
            pad = xT[:, :, :].rearrange("p k (b t) -> p k b t", t=TP)[:, :, :, T:TP]
            pool.memset(pad, 0.0).then_inc(consts, 1)
            pool.wait_ge(l_pos, 16)
            pool.wait_ge(l_tokb, 16)
            for j in range(NPT):
                if j == 3:
                    pool.wait_ge(l_pos_rest, 16)
                pool.tensor_tensor(posb[:, j, :], posb[:, j, :], tokb[:, :], ALU.add).then_inc(posb_done, 1)
            pool.memset(mask[:, :, :], 0.0).then_inc(mask_done, 1)
            pool.wait_ge(mask_done, 1)
            pool.affine_select(out=mask[:, :, :], in_=mask[:, :, :], compare_op=ALU.is_ge, fill=NEG, base=0,
                               pattern=[[0, HQ], [-1, TP]], channel_multiplier=1).then_inc(mask_done, 1)
            pool.wait_ge(norm_a, NPT)
            pool.wait_ge(cls_x, 1)
            pool.wait_ge(l_wproj, 16 * 2)
            pool.memset(vs, 1.0).then_inc(vs_ones, 1)
            pool.tensor_tensor(h0[:, :, :], h0[:, :, :], bp[:, :].unsqueeze(1).to_broadcast([P, NT, C]),
                               ALU.add).then_inc(bproj_done, 1)
            pool.tensor_tensor(h0c[:, :], h0c[:, :], bp[0:B, :], ALU.add).then_inc(bproj_done, 1)

            def take_queries(b, t, first=False):
                if not first:
                    pool.wait_ge(score_mm, b * 2 - 2)
                pool.tensor_copy(qs[:, t, :, :], qT[:, :, ds(b * TP, TP)]).then_inc(qs_done, 1)

            def build_kblk(b, f, first=False):
                if not first:
                    pool.wait_ge(score_mm, b * 2 + f - 1)
                pool.tensor_tensor(
                    kblk[:, f, :, :, :].rearrange("p c h k -> p (c h) k"),
                    kT[:, f, ds(b * TP, TP)].unsqueeze(1).to_broadcast([P, HH, TP]),
                    head_of_row[:, :].unsqueeze(2).to_broadcast([P, HH, TP]), ALU.mult).then_inc(kblk_done, 1)

            def take_values(b, t, first=False):
                if not first:
                    pool.wait_ge(pv_mm, b * 2 - 2)
                pool.tensor_copy(vs[:, t, :, 0:HD],
                                 v[:, ds(b, 1), :].rearrange("p o (h d) -> p (o h) d", d=HD))\
                    .then_inc(vs_done, 1)

            pool.wait_ge(patch_mm, NPT)
            pool.wait_ge(q_cp, 1)
            pool.wait_ge(k_cp, 1)
            take_queries(0, 0, first=True)
            take_queries(1, 1, first=True)
            build_kblk(0, 0, first=True)
            build_kblk(0, 1, first=True)
            pool.wait_ge(q_cp, NG)
            pool.wait_ge(k_cp, NG)
            pool.wait_ge(v_cpa, NG)
            pool.wait_ge(v_cpd, NG)
            pool.wait_ge(vs_ones, 1)
            take_values(0, 0, first=True)
            build_kblk(1, 0)
            build_kblk(1, 1)
            take_values(1, 1, first=True)
            with pool.Fori(1, B // 2) as i:
                for t in range(2):
                    b = i * 2 + t
                    take_queries(b, t)
                    build_kblk(b, 0)
                    build_kblk(b, 1)
                    take_values(b, t)

            y4 = yT[:, :, :].rearrange("p k (b t) -> p k b t", t=TP)

            def gather_ytile(n, slot, b0=0, b1=B, done=True):
                cp = pool.tensor_copy(ytile[:, slot, :, b0 * RT:b1 * RT].rearrange("p k (b s) -> p k b s", s=RT),
                                      y4[:, :, b0:b1, ds(n * RT - RT + 1, RT)])
                if done:
                    cp.then_inc(ytile_cp, 1)

            pool.wait_ge(yT_cp, B - 4)
            for n in range(1, 4):
                gather_ytile(n, n % 3, 0, B - 4, done=False)
            pool.wait_ge(yT_cp, B)
            for n in range(1, 4):
                gather_ytile(n, n % 3, B - 4, B)
            with pool.Fori(1, NT // 3) as i:
                for t in range(3):
                    pool.wait_ge(proj_mm, i * 3 + t - 1)
                    gather_ytile(i * 3 + t + 1, (t + 1) % 3)
            for n in range(NT // 3 * 3 + 1, NT + 1):
                pool.wait_ge(proj_mm, n - 2)
                gather_ytile(n, n % 3)

            pool.wait_ge(l_wall, 16)
            pool.wait_ge(r_dve, 11)

            def pick(b, t):
                e = pool.value_load(idx[0:1, ds(b, 1)], min_val=0, max_val=EXPERTS - 1)
                pool.tensor_copy(wsel[:, t:t + 1, WDN:WPK], wall[:, ds(e, 1), WDN:WPK]).then_inc(wup_cp, 1)

            for t in range(G):
                pick(t, t)
            with pool.Fori(1, NG) as i:
                for t in range(G):
                    pool.wait_ge(up_mm, i * G + t - G + 1)
                    pick(i * G + t, t)

        @block.scalar
        def _(act):
            act.dma_start(wt[:, 0:KX // 2, :], wtok[:, 0:KX // 2, :]).then_inc(l_wt[0], 16)
            act.dma_start(h0c[:, :], cls_tok).then_inc(l_cls, 16)
            act.dma_start(xhc[:, :], pos_cls).then_inc(l_cls, 16)
            act.dma_start(tokb[:, :], tok_b).then_inc(l_tokb, 16)
            act.dma_start(h0[:, NPT:NT, :], txt).then_inc(l_txt, 16)
            act.dma_start(colp[:, :, :], cols).then_inc(l_cols, 16)
            act.dma_start(wr[:, :, :], w_router).then_inc(l_cols, 16)
            act.dma_start(br[:, :], b_router).then_inc(l_cols, 16)
            act.dma_start(wlqv[:, :, :], w_lat_qv).then_inc(l_wattn, 16)
            act.dma_start(wlk[:, :, :], w_lat_k).then_inc(l_wattn, 16)
            act.dma_start(whq[:, :], w_heads_q).then_inc(l_wattn, 16)
            act.dma_start(whk[:, :], w_heads_k).then_inc(l_wattn, 16)
            act.dma_start(whv[LAT:P, :], w_heads_v).then_inc(l_wattn, 16)
            act.dma_start(wp[:, :, :], w_proj).then_inc(l_wproj, 16)
            act.dma_start(bp[:, :], b_proj).then_inc(l_wproj, 16)

            x4 = xT[:, :, :].rearrange("p k (b t) -> p k b t", t=TP)

            act.wait_ge(consts, FILLED)
            act.wait_ge(cls_dve, 3)
            act.activation(sd[0:B, 0, 0:1], mv[0:B, 0, 0, 1:2], ACT.Sqrt, bias=eps_col[0:B, :]).then_inc(cls_sqrt, 1)
            act.wait_ge(xpose_a, 1)
            act.copy(x4[:, :, :, 0:1].rearrange("p k b o -> p k (b o)"),
                     ps[:, 6, 0:KC * B].rearrange("p (k b) -> p k b", k=KC)).then_inc(xT_done, 1)

            def evac_tiles(j, t, with_txt=True):
                act.wait_ge(xpose_a, j + 2)
                for u, at in ((0, 1), (1, 1 + NPATCH)):
                    if u and not with_txt:
                        continue
                    last = act.copy(
                        x4[:, :, :, j * RT + at:(j + 1) * RT + at],
                        ps[:, 3 + t, 2 * u * P:2 * (u + 1) * P].rearrange("p (k b s) -> p k b s", k=KC, s=RT))
                last.then_inc(xT_done, 1)

            def deviations(j, t):
                act.wait_ge(aggr_a, j + 1)
                nu = 2 if j < NTT else 1
                act.activation(sd[:, t, 0:nu], mv[:, t, 0:nu, 1], ACT.Sqrt, bias=eps_col[:, :]).then_inc(sqrt_a, 1)

            for j in range(NPT):
                deviations(j, j % 3)
                if j:
                    evac_tiles(j - 1, (j - 1) % 3)
            evac_tiles(NPT - 1, (NPT - 1) % 3, with_txt=False)
            act.wait_ge(bn_dve, 1)
            act.activation(bn_tmp[:, :], bn_scale[:, :], ACT.Sqrt).then_inc(cls_sqrt, 1)

            def latqv_out(g, first=False):
                act.wait_ge(latqv_mm, g + 1)
                if not first:
                    act.wait_ge(q_mm, g)
                act.copy(latqv[:, :], ps[:, 0, 0:GN]).then_inc(latqv_cp, 1)

            def qv_out(g):
                act.wait_ge(v_mm, g * 2 + 2)
                act.copy(v[:, ds(g * G + 2, 2), :],
                         ps[0:TP, 7, :].rearrange("p (b n) -> p b n", b=2)).then_inc(v_cpa, 1)
                act.wait_ge(q_mm, g + 1)
                act.activation(qT[:, :, ds(g * GN, GN)], ps[:, 2:4, 0:GN], ACT.Copy,
                               scale=float(HD) ** -0.5).then_inc(q_cp, 1)

            latqv_out(0, first=True)
            with act.Fori(0, NG - 1) as i:
                act.wait_ge(v_mm, i * 2 + 2)
                act.copy(v[:, ds(i * G + 2, 2), :],
                         ps[0:TP, 7, :].rearrange("p (b n) -> p b n", b=2)).then_inc(v_cpa, 1)
                latqv_out(i + 1)
                act.wait_ge(q_mm, i + 1)
                act.activation(qT[:, :, ds(i * GN, GN)], ps[:, 2:4, 0:GN], ACT.Copy,
                               scale=float(HD) ** -0.5).then_inc(q_cp, 1)
            qv_out(NG - 1)

            def exps(b, f, first=False):
                n = b * 2 + f
                if not first:
                    act.wait_ge(pv_mm, n - 1)
                for c in range(2):
                    act.wait_ge(prob_xp, n * 2 + c + 1)
                    act.activation(prob[:, f, c, :, :].rearrange("p h n -> p (h n)"), ps[0:TP, 4 + c, 0:HC],
                                   ACT.Exp).then_inc(exp_done, 1)

            def yraw_out(b, f, first=False):
                n = b * 2 + f
                act.wait_ge(pv_mm, n + 1)
                if not first:
                    act.wait_ge(yraw_xp, n - 1)
                act.copy(yraw[:, f, :, :].rearrange("p c n -> p (c n)"),
                         ps[:, 6, f * 2 * TP:(f + 1) * 2 * TP]).then_inc(yraw_cp, 1)

            def yT_out(b):
                act.wait_ge(yT_xp, b + 1)
                act.copy(yT[:, :, ds(b * TP, TP)],
                         ps[:, 6, HC:HC + KC * TP].rearrange("p (k n) -> p k n", k=KC)).then_inc(yT_cp, 1)

            act.wait_ge(patch_mm, NPT)
            exps(0, 0, first=True)
            exps(0, 1, first=True)
            yraw_out(0, 0, first=True)
            exps(1, 0)
            yraw_out(0, 1, first=True)
            exps(1, 1)
            yraw_out(1, 0)
            with act.Fori(1, B // 2) as i:
                for t in range(2):
                    b = i * 2 + t
                    exps(b, 0)
                    yraw_out(b - 1, 1)
                    yT_out(b - 2)
                    exps(b, 1)
                    yraw_out(b, 0)
            yraw_out(B - 1, 1)
            yT_out(B - 2)
            yT_out(B - 1)

            z4 = zT[:, :, :].rearrange("p k (b t) -> p k b t", t=TP)
            r4 = h1T[:, :, :].rearrange("p k (b t) -> p k b t", t=TP)

            def deviation_c(n, s, rows):
                act.wait_ge(aggr_c, n + 1)
                act.activation(sd[0:rows, s, 0:1], mv[0:rows, s, 0, 1:2], ACT.Sqrt, bias=eps2_col[0:rows, :],
                               scale=1.0 + EPS).then_inc(sqrt_c, 1)

            def evac_c(n, s, at, cnt):
                act.wait_ge(xpose_c, n + 1)
                for k in range(KC):
                    act.activation(z4[:, k, :, ds(at, cnt)],
                                   ps[:, XP[s], k * B * cnt:(k + 1) * B * cnt].rearrange("p (b s) -> p b s", s=cnt),
                                   ACT.Identity, bias=colp[:, 1, k:k + 1], scale=colp[:, 0, k:k + 1])\
                        .then_inc(zT_cp, 1)
                src = ps[:, XP[s], C:C + KC * B * cnt].rearrange("p (k b s) -> p k b s", k=KC, s=cnt)
                if cnt == 1:
                    act.copy(r4[:, :, :, 0], src[:, :, :, 0]).then_inc(h1T_cp, 1)
                else:
                    act.copy(r4[:, :, :, ds(at, cnt)], src).then_inc(h1T_cp, 1)

            deviation_c(0, 0, B)
            deviation_c(1, 1, P)
            evac_c(0, 0, 0, 1)
            deviation_c(2, 2, P)
            evac_c(1, 1, 1, RT)
            with act.Fori(1, (NT + 1) // 3) as i:
                for t in range(3):
                    deviation_c(i * 3 + t, t, P)
                    evac_c(i * 3 + t - 1, (t + 2) % 3, (i * 3 + t) * RT - 2 * RT + 1, RT)
            evac_c(NT, NT % 3, (NT - 1) * RT + 1, RT)

            act.wait_ge(r_dve, 4)
            act.activation(ex[:, :], lg[:, :], ACT.Exp, bias=ntop[:, :], accum_out=exs[:, :]).then_inc(r_act, 1)

            act.wait_ge(hid_ones, 1)

            def relu(b, t, first=False):
                act.wait_ge(down_mm, b + 1)
                if not first:
                    act.wait_ge(up_mm, b - G + 1)
                act.activation(hid[0:HID, t, :], ps[0:HID, t % 2, 0:T], ACT.Relu,
                               bias=wsel[0:HID, t, WDN - 1:WDN]).then_inc(relu_done, 1)

            for t in range(G):
                relu(t, t, first=True)
            with act.Fori(1, NG) as i:
                for t in range(G):
                    relu(i * G + t, t)

        @block.tensor
        def _(pe):
            def products(j, t, turn, first=False):
                pe.wait_ge(l_x[t], turn * 16 + 16)
                if not first:
                    pe.wait_ge(h_added, j - 2)
                for k in range(KX):
                    if j == 0 and k % (KX // 2) == 0:
                        pe.wait_ge(l_wt[k // (KX // 2)], 16)
                    last = nc.tensor.matmul(ps[:, t, 0:C], xin[:, t, k, :], wt[:, k, :], start=(k == 0),
                                            stop=(k == KX - 1))
                last.then_inc(patch_mm, 1)

            def transposes(j, t, first=False, with_txt=True):
                pe.wait_ge(norm_a, j + 1)
                if not first:
                    pe.wait_ge(xT_done, j - 1)
                for u in range(2 if with_txt else 1):
                    for k in range(KC):
                        c = (2 * u + k) * P
                        last = nc.tensor.transpose(ps[:, 3 + t, c:c + P], xh[:, t, u, k * P:(k + 1) * P],
                                                   ident[:, :])
                last.then_inc(xpose_a, 1)

            for j in range(NPT):
                products(j, j % 3, j // 3, first=(j < 3))
                if j == 0:
                    pe.wait_ge(consts, IDENTITIES)
                    pe.wait_ge(cls_x, 1)
                    for k in range(KC):
                        last = nc.tensor.transpose(ps[:, 6, k * B:(k + 1) * B], xhc[:, k * P:(k + 1) * P],
                                                   ident[0:B, 0:B])
                    last.then_inc(xpose_a, 1)
                else:
                    transposes(j - 1, (j - 1) % 3, first=(j < 4))
            transposes(NPT - 1, (NPT - 1) % 3, with_txt=False)

            def latents(g, first=False):
                cols_ = ds(g * GN, GN)
                if not first:
                    pe.wait_ge(latqv_cp, g)
                for k in range(KC):
                    last = nc.tensor.matmul(ps[:, 0, 0:GN], wlqv[:, k, :], xT[:, k, cols_], start=(k == 0),
                                            stop=(k == KC - 1))
                last.then_inc(latqv_mm, 1)
                if not first:
                    pe.wait_ge(latk_cp, g)
                for k in range(KC):
                    last = nc.tensor.matmul(ps[:, 1, 0:GN], wlk[:, k, :], xT[:, k, cols_], start=(k == 0),
                                            stop=(k == KC - 1))
                last.then_inc(latk_mm, 1)

            def heads(g, first=False):
                pe.wait_ge(latqv_cp, g + 1)
                for u in range(2):
                    if not first:
                        pe.wait_ge((v_cpd, v_cpa)[u], g)
                    for w in range(2):
                        s = 2 * u + w
                        last = nc.tensor.matmul(ps[0:TP, 6 + u, w * C:(w + 1) * C],
                                                latqv[LAT:P, s * TP:(s + 1) * TP], whv[LAT:P, :],
                                                start=True, stop=True)
                    last.then_inc(v_mm, 1)
                if not first:
                    pe.wait_ge(q_cp, g)
                for k in range(KC):
                    last = nc.tensor.matmul(ps[:, 2 + k, 0:GN], whq[:, k * P:(k + 1) * P], latqv[0:LAT, :],
                                            start=True, stop=True)
                last.then_inc(q_mm, 1)
                pe.wait_ge(latk_cp, g + 1)
                if not first:
                    pe.wait_ge(k_cp, g)
                for k in range(KC):
                    last = nc.tensor.matmul(ps[:, 4 + k, 0:GN], whk[:, k * P:(k + 1) * P], latk[0:LAT, :],
                                            start=True, stop=True)
                last.then_inc(k_mm, 1)

            pe.wait_ge(l_wattn, 16 * 5)
            pe.wait_ge(xT_done, NPT + 1)
            pe.wait_ge(consts, PADDING)
            latents(0, first=True)
            latents(1)
            heads(0, first=True)
            with pe.Fori(1, NG - 1) as i:
                latents(i + 1)
                heads(i)
            heads(NG - 1)

            def scores(b, f, t, first=False):
                n = b * 2 + f
                if f == 0:
                    pe.wait_ge(qs_done, b + 1)
                pe.wait_ge(kblk_done, n + 1)
                if not first:
                    pe.wait_ge(sub_done, n - 1)
                for c in range(2):
                    bank = ps[0:TP, 2 * f + c, 0:HC]
                    nc.tensor.matmul(bank, ident_bf[:, :], mask[:, :, :].rearrange("p h k -> p (h k)"),
                                     start=True, stop=False)
                    last = nc.tensor.matmul(bank, qs[:, t, f, :],
                                            kblk[:, f, c, :, :].rearrange("p h k -> p (h k)"), start=False,
                                            stop=True)
                last.then_inc(score_mm, 1)

            def prob_transposes(b, f, first=False):
                n = b * 2 + f
                pe.wait_ge(sub_done, n + 1)
                for c in range(2):
                    if not first:
                        pe.wait_ge(exp_done, n * 2 - 1 + c)
                    for h in range(HQ):
                        last = nc.tensor.transpose(ps[0:TP, 4 + c, h * TP:(h + 1) * TP], dif[:, f, c, h, :],
                                                   ident[0:TP, 0:TP])
                    last.then_inc(prob_xp, 1)

            def weighted_values(b, f, t, first=False, after_y=False):
                n = b * 2 + f
                pe.wait_ge(exp_done, n * 2 + 2)
                if f == 0:
                    pe.wait_ge(vs_done, b + 1)
                if not first:
                    pe.wait_ge(yraw_cp, n)
                if after_y:
                    pe.wait_ge(yT_cp, b - 1)
                for c in range(2):
                    for h in range(HQ):
                        last = nc.tensor.matmul(ps[h * VS:(h + 1) * VS, 6, (2 * f + c) * TP:(2 * f + c + 1) * TP],
                                                vs[:, t, f * HH + c * HQ + h, :], prob[:, f, c, h, :],
                                                start=True, stop=True, tile_position=(0, h * VS),
                                                skip_group_check=True)
                last.then_inc(pv_mm, 1)

            def yraw_transposes(b, f, first=False):
                n = b * 2 + f
                pe.wait_ge(yraw_cp, n + 1)
                if not first:
                    pe.wait_ge(ynorm, b)
                for c in range(2):
                    at = (2 * f + c) * P
                    last = nc.tensor.transpose(ps[0:TP, 7, at:at + P], yraw[:, f, c, :], ident[:, :])
                last.then_inc(yraw_xp, 1)

            def y_transposes(b, last=False):
                pe.wait_ge(ynorm, b + 1)
                pe.wait_ge(yraw_cp, b * 2 + (2 if last else 4))
                for k in range(KC):
                    done = nc.tensor.transpose(ps[:, 6, HC + k * TP:HC + (k + 1) * TP],
                                               yn[:, k * P:(k + 1) * P], ident[0:TP, 0:TP])
                done.then_inc(yT_xp, 1)

            def attend(b, t, end=False):
                early = b if isinstance(b, int) else 4
                scores(b, 1, t, first=(early == 0))
                prob_transposes(b, 0, first=(early == 0))
                if early > 0:
                    weighted_values(b - 1, 1, 1 - t)
                    yraw_transposes(b - 1, 0, first=(early == 1))
                if not end:
                    scores(b + 1, 0, 1 - t)
                if early > 1:
                    y_transposes(b - 2)
                prob_transposes(b, 1)
                weighted_values(b, 0, t, first=(early == 0), after_y=(early > 1))
                if early > 0:
                    yraw_transposes(b - 1, 1, first=(early == 1))

            pe.wait_ge(mask_done, 2)
            pe.wait_ge(latqv_cp, NG)
            pe.wait_ge(latk_cp, NG)
            scores(0, 0, 0, first=True)
            pe.wait_ge(q_cp, NG)
            pe.wait_ge(k_cp, NG)
            pe.wait_ge(v_cpa, NG)
            pe.wait_ge(v_cpd, NG)
            for b in range(4):
                attend(b, b % 2)
            with pe.Fori(2, B // 2 - 1) as i:
                for t in range(2):
                    attend(i * 2 + t, t)
            for b in range(B - 2, B):
                attend(b, b % 2, end=(b + 1 == B))
            weighted_values(B - 1, 1, 1)
            yraw_transposes(B - 1, 0)
            y_transposes(B - 2)
            yraw_transposes(B - 1, 1)
            pe.wait_ge(yT_cp, B - 1)
            y_transposes(B - 1, last=True)

            y4 = yT[:, :, :].rearrange("p k (b t) -> p k b t", t=TP)

            def project(n, s, cls=False):
                rows = B if cls else P
                if not cls:
                    pe.wait_ge(ytile_cp, n)
                for k in range(KC):
                    lhsT = y4[:, k, :, 0] if cls else ytile[:, s, k, :]
                    last = nc.tensor.matmul(ps[0:rows, PROJ[s], 0:C], lhsT, wp[:, k, :], start=(k == 0),
                                            stop=(k == KC - 1))
                last.then_inc(proj_mm, 1)

            def ln2_out(n, s, cls=False, end=False):
                rows = B if cls else P
                pe.wait_ge(zh_done, n + 1)
                for k in range(KC):
                    nc.tensor.transpose(ps[:, XP[s], k * rows:(k + 1) * rows], zh[0:rows, s, k * P:(k + 1) * P],
                                        ident[0:rows, 0:rows])
                for k in range(KC):
                    nc.tensor.transpose(ps[:, XP[s], C + k * rows:C + (k + 1) * rows], h1[0:rows, s, k * P:(k + 1) * P],
                                        ident[0:rows, 0:rows])
                for k in range(KC):
                    last = nc.tensor.matmul(ps[:, 4 + k, 0:B], zh[0:rows, s, k * P:(k + 1) * P],
                                            ident[0:B, 0:B] if cls else seq_of_row[:, :], start=cls, stop=end,
                                            skip_group_check=True)
                last.then_inc(xpose_c, 1)

            pe.wait_ge(yT_cp, B)
            pe.wait_ge(l_wproj, 32)
            project(0, 0, cls=True)
            project(1, 1)
            project(2, 2)
            ln2_out(0, 0, cls=True)

            def out_step(n, s, first=False):
                pe.wait_ge(h1_done, n - 2)
                project(n, s)
                if not first:
                    pe.wait_ge(h1T_cp, n - 4)
                ln2_out(n - 2, (s + 1) % 3)

            for n in range(3, 6):
                out_step(n, n % 3, first=(n < 5))
            with pe.Fori(2, (NT + 1) // 3) as i:
                for t in range(3):
                    out_step(i * 3 + t, t)
            for n in range(NT - 1, NT + 1):
                pe.wait_ge(h1T_cp, n - 2)
                ln2_out(n, n % 3, end=(n == NT))

            pe.wait_ge(r_dve, 1)
            for k in range(KC):
                last = nc.tensor.matmul(ps[0:B, 0, 0:EXPERTS], zbn[:, k, :], wr[:, k, :], start=(k == 0),
                                        stop=(k == KC - 1))
            last.then_inc(r_logit, 1)
            pe.wait_ge(r_dve, 10)
            nc.tensor.matmul(ps[:, 4, 0:B], gate_col[:, :], ident[0:B, 0:B], start=True, stop=True)
            nc.tensor.matmul(ps[0:1, 5, 0:B], idx_col[:, :], ident[0:B, 0:B], start=True, stop=True)\
                .then_inc(r_bcast, 1)

            def down(b, t):
                for k in range(KC):
                    last = nc.tensor.matmul(ps[0:HID, t % 2, 0:T], wsel[:, t, k * HID:(k + 1) * HID],
                                            zT[:, k, ds(b * TP, T)], start=(k == 0), stop=(k == KC - 1))
                last.then_inc(down_mm, 1)

            def up(b, t):
                for k in range(KC):
                    c = WDN + k * P
                    last = nc.tensor.matmul(ps[:, 2 + t % 2, k * T:(k + 1) * T], wsel[0:HID + 1, t, c:c + P],
                                            hid[:, t, :], start=True, stop=True)
                last.then_inc(up_mm, 1)

            def ffn_step(b, t, first=False, end=False):
                if not end:
                    pe.wait_ge(wdown_cp, b + 3)
                pe.wait_ge(wup_cp, b + 1)
                if not first:
                    pe.wait_ge(out_done, b - 1)
                pe.wait_ge(relu_done, b + 1)
                up(b, t)
                if not end:
                    down(b + 2, (t + 2) % G)

            pe.wait_ge(h1T_cp, NT + 1)
            for b in range(2):
                pe.wait_ge(wdown_cp, b + 1)
                down(b, b)
            for b in range(G):
                ffn_step(b, b, first=(b < 2))
            with pe.Fori(1, NG - 1) as i:
                for t in range(G):
                    ffn_step(i * G + t, t)
            for b in range(B - G, B):
                ffn_step(b, b % G, end=(b + 2 >= B))

        @block.vector
        def _(dve):
            nc.vector.memset(hid[HID:HID + 1, :, :], 1.0).then_inc(hid_ones, 1)
            dve.wait_ge(l_cls, 32)
            nc.vector.tensor_tensor(h0c[:, :], h0c[:, :], xhc[:, :], ALU.add).then_inc(cls_dve, 1)
            dve.wait_ge(cls_dve, 1)
            nc.vector.bn_stats(st[0:B, 0, 0, :], h0c[:, :]).then_inc(cls_dve, 1)
            dve.wait_ge(cls_dve, 2)
            nc.vector.bn_aggr(mv[0:B, 0, 0, :], st[0:B, 0, 0, :]).then_inc(cls_dve, 1)
            dve.wait_ge(cls_sqrt, 1)
            nc.vector.reciprocal(rs[0:B, 0, 0:1], sd[0:B, 0, 0:1]).then_inc(cls_dve, 1)
            dve.wait_ge(cls_dve, 4)
            nc.vector.tensor_scalar(xhc[:, :], h0c[:, :], mv[0:B, 0, 0, 0:1], rs[0:B, 0, 0:1], ALU.subtract,
                                    ALU.mult).then_inc(cls_x, 1)

            def ln1(j, t, first=False, with_txt=True):
                nu = 2 if with_txt else 1
                if with_txt:
                    nc.vector.bn_stats(st[:, t, 1, :], h0[:, j + NPT, :])
                dve.wait_ge(posb_done, j + 1)
                dve.wait_ge(patch_mm, j + 1)
                nc.vector.tensor_tensor(h0[:, j, :], ps[:, t, 0:C], posb[:, j, :], ALU.add).then_inc(h_added, 1)
                dve.wait_ge(h_added, j + 1)
                nc.vector.bn_stats(st[:, t, 0, :], h0[:, j, :]).then_inc(stats_a, 1)
                dve.wait_ge(stats_a, j + 1)
                for u in range(nu):
                    last = nc.vector.bn_aggr(mv[:, t, u, :], st[:, t, u, :])
                last.then_inc(aggr_a, 1)
                dve.wait_ge(sqrt_a, j + 1)
                nc.vector.reciprocal(rs[:, t, 0:nu], sd[:, t, 0:nu]).then_inc(recip_a, 1)
                dve.wait_ge(recip_a, j + 1)
                if not first:
                    dve.wait_ge(xpose_a, j - 1)
                for u in range(nu):
                    last = nc.vector.tensor_scalar(xh[:, t, u, :], h0[:, j + u * NPT, :], mv[:, t, u, 0:1], rs[:, t, u:u + 1],
                                                   ALU.subtract, ALU.mult)
                last.then_inc(norm_a, 1)

            dve.wait_ge(cls_x, 1)
            dve.wait_ge(l_txt, 16)
            for j in range(NPT):
                ln1(j, j % 3, first=(j < 3), with_txt=(j < NTT))
            dve.wait_ge(l_cols, 48)
            nc.vector.tensor_scalar(bn_scale[:, :], colp[:, 5, :], EPS, None, ALU.add).then_inc(bn_dve, 1)

            def latk_out(g, first=False):
                dve.wait_ge(latk_mm, g + 1)
                if not first:
                    dve.wait_ge(k_mm, g)
                nc.vector.tensor_copy(latk[0:LAT, :], ps[0:LAT, 1, 0:GN]).then_inc(latk_cp, 1)

            def kv_out(g):
                dve.wait_ge(v_mm, g * 2 + 1)
                nc.vector.tensor_copy(v[:, ds(g * G, 2), :],
                                      ps[0:TP, 6, :].rearrange("p (b n) -> p b n", b=2))\
                    .then_inc(v_cpd, 1)
                dve.wait_ge(k_mm, g + 1)
                nc.vector.tensor_copy(kT[:, :, ds(g * GN, GN)], ps[:, 4:6, 0:GN]).then_inc(k_cp, 1)

            latk_out(0, first=True)
            dve.wait_ge(cls_sqrt, 2)
            nc.vector.reciprocal(bn_scale[:, :], bn_tmp[:, :]).then_inc(bn_dve, 1)
            dve.wait_ge(bn_dve, 2)
            nc.vector.tensor_tensor(bn_scale[:, :], bn_scale[:, :], colp[:, 2, :], ALU.mult).then_inc(bn_dve, 1)
            nc.vector.tensor_tensor(zs_shift[:, :], colp[:, 1, :], colp[:, 4, :], ALU.subtract).then_inc(bn_dve, 1)
            dve.wait_ge(bn_dve, 4)
            nc.vector.scalar_tensor_tensor(zs_scale[:, :], bn_scale[:, :], 1.0 / T, colp[:, 0, :], ALU.mult,
                                           ALU.mult).then_inc(bn_dve, 1)
            nc.vector.tensor_tensor(bn_tmp[:, :], zs_shift[:, :], bn_scale[:, :], ALU.mult).then_inc(bn_dve, 1)
            dve.wait_ge(bn_dve, 6)
            nc.vector.tensor_tensor(zs_shift[:, :], bn_tmp[:, :], colp[:, 3, :], ALU.add).then_inc(bn_dve, 1)
            with dve.Fori(0, NG - 1) as i:
                kv_out(i)
                latk_out(i + 1)
            kv_out(NG - 1)

            def shift(b, f, first=False):
                n = b * 2 + f
                scores_ = ps[0:TP, 2 * f:2 * f + 2, 0:HC].rearrange("p c (h k) -> p c h k", k=TP)
                dve.wait_ge(score_mm, n + 1)
                nc.vector.tensor_reduce(mx[:, f, :, :], scores_, AX_X, ALU.max).then_inc(max_done, 1)
                dve.wait_ge(max_done, n + 1)
                if not first:
                    dve.wait_ge(prob_xp, n * 2 - 2)
                nc.vector.tensor_tensor(dif[:, f, :, :, :], scores_,
                                        mx[:, f, :, :].unsqueeze(3).to_broadcast([TP, 2, HQ, TP]),
                                        ALU.subtract).then_inc(sub_done, 1)

            def normalise(b, first=False):
                o = ps[0:TP, 7, :].rearrange("p (h d) -> p h d", d=VS)
                dve.wait_ge(yraw_xp, b * 2 + 2)
                nc.vector.reciprocal(rc[:, :], o[:, :, HD]).then_inc(rec_done, 1)
                dve.wait_ge(rec_done, b + 1)
                if not first:
                    dve.wait_ge(yT_xp, b)
                nc.vector.tensor_tensor(yn[:, :].rearrange("p (h d) -> p h d", d=HD), o[:, :, 0:HD],
                                        rc[:, :].unsqueeze(2).to_broadcast([TP, HEADS, HD]), ALU.mult)\
                    .then_inc(ynorm, 1)

            dve.wait_ge(patch_mm, NPT)
            for b in range(4):
                shift(b, 0, first=(b == 0))
                if b > 1:
                    normalise(b - 2, first=(b == 2))
                shift(b, 1, first=(b == 0))
            with dve.Fori(2, B // 2) as i:
                for t in range(2):
                    b = i * 2 + t
                    shift(b, 0)
                    normalise(b - 2)
                    shift(b, 1)
            normalise(B - 2)
            normalise(B - 1)

            def add_residual(n, s, j, cls=False):
                rows = B if cls else P
                old = h0c[:, :] if cls else h0[:, ds(j, 1), :].rearrange("p o n -> p (o n)")
                dve.wait_ge(proj_mm, n + 1)
                nc.vector.tensor_tensor(h1[0:rows, s, :], ps[0:rows, PROJ[s], 0:C], old, ALU.add).then_inc(h1_done, 1)

            def take_stats(n, s, rows=P):
                dve.wait_ge(h1_done, n + 1)
                nc.vector.bn_stats(st[0:rows, s, 0, :], h1[0:rows, s, :]).then_inc(stats_c, 1)

            def merge_stats(s, rows=P):
                nc.vector.bn_aggr(mv[0:rows, s, 0, :], st[0:rows, s, 0, :]).then_inc(aggr_c, 1)

            def invert(n, s, rows=P):
                dve.wait_ge(sqrt_c, n + 1)
                nc.vector.reciprocal(rs[0:rows, s, 0:1], sd[0:rows, s, 0:1]).then_inc(recip_c, 1)

            def standardise(n, s, rows=P):
                dve.wait_ge(recip_c, n + 1)
                nc.vector.tensor_scalar(zh[0:rows, s, :], h1[0:rows, s, :], mv[0:rows, s, 0, 0:1],
                                        rs[0:rows, s, 0:1], ALU.subtract, ALU.mult).then_inc(zh_done, 1)

            def ln2_step(n, s, before=P):
                add_residual(n, s, n - 1)
                invert(n - 1, (s + 2) % 3, before)
                take_stats(n, s)
                dve.wait_ge(stats_c, n + 1)
                standardise(n - 1, (s + 2) % 3, before)
                merge_stats(s)

            dve.wait_ge(bproj_done, 2)
            add_residual(0, 0, 0, cls=True)
            take_stats(0, 0, B)
            dve.wait_ge(stats_c, 1)
            merge_stats(0, B)
            ln2_step(1, 1, before=B)
            ln2_step(2, 2)
            with dve.Fori(1, (NT + 1) // 3) as i:
                for t in range(3):
                    n = i * 3 + t
                    dve.wait_ge(xpose_c, n - 2)
                    ln2_step(n, t)
            invert(NT, NT % 3)
            standardise(NT, NT % 3)

            dve.wait_ge(xpose_c, NT + 1)
            for k in range(KC):
                last = nc.vector.tensor_scalar(zbn[:, k, :], ps[:, 4 + k, 0:B], zs_scale[:, k:k + 1],
                                               zs_shift[:, k:k + 1], ALU.mult, ALU.add)
            last.then_inc(r_dve, 1)
            dve.wait_ge(r_logit, 1)
            nc.vector.tensor_tensor(lg[:, :], ps[0:B, 0, 0:EXPERTS], br[:, :], ALU.add).then_inc(r_dve, 1)
            dve.wait_ge(r_dve, 2)
            nc.vector.max(top[:, :], lg[:, :]).then_inc(r_dve, 1)
            dve.wait_ge(r_dve, 3)
            nc.vector.tensor_scalar(ntop[:, :], top[:, 0:1], -1.0, None, ALU.mult).then_inc(r_dve, 1)
            dve.wait_ge(r_act, 1)
            nc.vector.reciprocal(exr[:, :], exs[:, :]).then_inc(r_dve, 1)
            dve.wait_ge(r_dve, 5)
            nc.vector.tensor_scalar(pr[:, :], ex[:, :], exr[:, 0:1], None, ALU.mult).then_inc(r_dve, 1)
            dve.wait_ge(r_dve, 6)
            nc.vector.max(ptop[:, :], pr[:, :]).then_inc(r_dve, 1)
            dve.wait_ge(r_dve, 7)
            nc.vector.max_index(pidx[:, :], ptop[:, :], pr[:, :]).then_inc(r_dve, 1)
            dve.wait_ge(r_dve, 8)
            nc.vector.tensor_copy(idx_col[:, :], pidx[:, 0:1]).then_inc(r_dve, 1)
            nc.vector.tensor_copy(gate_col[:, :], ptop[:, 0:1].to_broadcast([B, P])).then_inc(r_dve, 1)
            dve.wait_ge(r_bcast, 1)
            nc.vector.tensor_copy(idx[:, :], ps[0:1, 5, 0:B]).then_inc(r_dve, 1)
            nc.vector.tensor_copy(gate[:, :], ps[:, 4, 0:B]).then_inc(r_dve, 1)

            def finish(b, g, t):
                dve.wait_ge(up_mm, b + 1)
                nc.vector.scalar_tensor_tensor(
                    oT[:, ds(g, 1), :, t * T:(t + 1) * T].rearrange("p o k n -> p (o k) n"),
                    ps[:, 2 + t % 2, 0:KC * T].rearrange("p (k n) -> p k n", k=KC), gate[:, ds(b, 1)],
                    h1T[:, :, ds(b * TP, T)], ALU.mult, ALU.add).then_inc(out_done, 1)

            def pick(b, t):
                e = dve.value_load(idx[0:1, ds(b, 1)], min_val=0, max_val=EXPERTS - 1)
                nc.vector.tensor_copy(wsel[:, t:t + 1, 0:WDN], wall[:, ds(e, 1), 0:WDN]).then_inc(wdown_cp, 1)

            dve.wait_ge(l_wall, 16)
            dve.wait_ge(r_dve, 12)
            for t in range(G):
                pick(t, t)
            dve.wait_ge(h1T_cp, NT + 1)
            with dve.Fori(0, NG - 1) as i:
                for t in range(G):
                    finish(i * G + t, i, t)
                    dve.wait_ge(relu_done, i * G + t + 1)
                    pick(i * G + t + G, t)
            for t in range(G):
                finish(B - G + t, NG - 1, t)


_OUT = (NG, P, KC * G * T)


def kernel(**inputs):
    import concourse.bacc as bacc
    from concourse.bass_utils import run_bass_kernel_spmd as run

    a = {k: np.asarray(v) for k, v in inputs.items()}
    con = np.ascontiguousarray

    x = a["x"].reshape(B, 3, 6, 16, 6, 16).transpose(0, 2, 4, 1, 3, 5).reshape(B, NPT, RT, KX, P)
    patches = x.transpose(1, 4, 3, 0, 2).reshape(NPT, P, KX, P)
    tiled = lambda w: w.reshape(-1, P, w.shape[-1]).transpose(1, 0, 2)
    pos = a["L0_tok_pos_embedding"][0]
    pos_rows = np.broadcast_to(pos[1:1 + NPATCH].reshape(NPT, RT, C).transpose(1, 0, 2), (B, RT, NPT, C))
    rows = lambda r, n: np.broadcast_to(r.reshape(1, -1), (n, r.size))
    col = lambda r: r.reshape(KC, P).T
    up_ = np.zeros((EXPERTS, P, C), np.float32)
    up_[:, 0:HID] = a["L0_ffn_W_up"]
    up_[:, HID] = a["L0_ffn_b_up"]
    bd = np.zeros((EXPERTS, P, 1), np.float32)
    bd[:, 0:HID, 0] = a["L0_ffn_b_down"]
    down_ = a["L0_ffn_W_down"].reshape(EXPERTS, KC, P, HID).transpose(0, 2, 1, 3).reshape(EXPERTS, P, KC * HID)
    arrays = dict(
        patches=patches, wtok=tiled(a["L0_tok_W"].T),
        txt=a["txt"].reshape(B, NTT, RT, C).transpose(0, 2, 1, 3).reshape(P, NTT, C),
        pos_rows=pos_rows.reshape(P, NPT, C), tok_b=rows(a["L0_tok_b"], P),
        cls_tok=rows(a["L0_tok_class_token"], B), pos_cls=rows(pos[0], B),
        w_lat_qv=tiled(np.concatenate([a["L0_attn_wq_lat"], a["L0_attn_wv_lat"]], 1)),
        w_lat_k=tiled(np.concatenate([a["L0_attn_wk_lat"]] * 2, 1)), w_heads_q=a["L0_attn_wq_heads"], w_heads_k=a["L0_attn_wk_heads"],
        w_heads_v=a["L0_attn_wv_heads"], w_proj=tiled(a["L0_attn_w_proj"]), b_proj=rows(a["L0_attn_b_proj"], P),
        cols=np.stack([col(a["L0_ffn_" + n]) for n in ("ln_g", "ln_b", "bn_g", "bn_b", "bn_mean", "bn_var")], 1),
        w_router=tiled(a["L0_ffn_Wr"]), b_router=rows(a["L0_ffn_br"], B),
        experts=np.concatenate([down_, bd, up_], 2).transpose(1, 0, 2))

    nc = bacc.Bacc("TRN2", target_bir_lowering=False, num_devices=1)
    arrays = {f"in_{k}": con(v) for k, v in arrays.items()}
    args = [nc.dram_tensor(k, v.shape, F32, kind="ExternalInput").ap() for k, v in arrays.items()]
    out = nc.dram_tensor("out_rows", _OUT, F32, kind="ExternalOutput").ap()
    early_fusion(nc, *args, out)
    r = run(nc, [arrays], core_ids=[0])
    got = np.asarray(r.results[0]["out_rows"])
    got = got.reshape(NG, P, KC, G, T).transpose(0, 3, 4, 2, 1)
    return con(got.reshape(B, T, C))
```

```python
from contextlib import ExitStack

import numpy as np

import concourse.bass as bass
from concourse import mybir

ALU = mybir.AluOpType
ACT = mybir.ActivationFunctionType
F32 = mybir.dt.float32
BF16 = mybir.dt.bfloat16
I32 = mybir.dt.int32
U32 = mybir.dt.uint32
AX_X = mybir.AxisListType.X
ds = bass.ds

P = 128
B = 32
NPATCH, NTXT = 36, 32
T = 1 + NPATCH + NTXT
TP = T + 1
C = 256
KC = C // P
KX = 3 * 16 * 16 // P
RT = 4
NPT, NTT = NPATCH // RT, NTXT // RT
NT = NPT + NTT
assert (NT + 1) % 3 == 0
HEADS, HD, LAT = 16, 16, 64
HH = P // HD
HQ = 4
HC = HQ * TP
XS = 4
VS = P // HQ
G = 4
GN = G * TP
NG = B // G
EXPERTS, HID = 8, 64
EPS = 1e-5
NEG = -1e30
WDN = KC * HID + 1
WPK = WDN + C


def early_fusion(nc, patches, wtok, txt, pos_rows, tok_b, cls_tok, pos_cls, w_lat_qv, w_lat_k, w_heads_q,
                 w_heads_k, w_heads_v, w_proj, b_proj, cols, w_router, b_router, experts, out):
    with ExitStack() as ctx:
        def sb(name, shape, dt=F32):
            return ctx.enter_context(nc.sbuf_tensor(name, shape, dt))

        def sem(name):
            return ctx.enter_context(nc.semaphore(name))

        ident = sb("ident", [P, P])
        ident_bf = sb("ident_bf", [TP, TP], BF16)
        mask = sb("mask", [TP, HQ, TP], BF16)
        head_of_row = sb("head_of_row", [P, HH])
        seq_of_row = sb("seq_of_row", [P, B])
        h0 = sb("h0", [P, NT, C])
        h0c = sb("h0c", [B, C])
        xT = sb("xT", [P, KC, B * TP])
        qT = sb("qT", [P, KC, B * TP])
        kT = sb("kT", [P, KC, B * TP])
        yT = sb("yT", [P, KC, B * TP])
        v = sb("v", [TP, B, C])
        res = v
        zT = xT
        wlqv = sb("wlqv", [P, KC, P])
        wlk = sb("wlk", [P, KC, P])
        whq = sb("whq", [LAT, C])
        whk = sb("whk", [LAT, C])
        whv = sb("whv", [P, C])
        latqv = sb("latqv", [P, GN])
        latk = sb("latk", [P, GN])
        wp = sb("wp", [P, KC, C])
        bp = sb("bp", [P, C])
        tokb = sb("tokb", [P, C])
        colp = sb("colp", [P, 6, KC])
        eps_col = sb("eps_col", [P, 1])
        eps2_col = sb("eps2_col", [P, 1])
        bn_scale = sb("bn_scale", [P, KC])
        bn_tmp = sb("bn_tmp", [P, KC])
        zs_scale = sb("zs_scale", [P, KC])
        zs_shift = sb("zs_shift", [P, KC])
        wr = sb("wr", [P, KC, EXPERTS])
        br = sb("br", [1, EXPERTS])
        wall = sb("wall", [P, EXPERTS, WPK])
        wsel = sb("wsel", [P, G, WPK])
        hid = sb("hid", [P, G, T])
        xh = sb("xh", [P, 3, 2, C])
        xhc = sb("xhc", [B, C])
        st = sb("st", [P, 3, 2, 6])
        mv = sb("mv", [P, 3, 2, 2])
        sd = sb("sd", [P, 3, 2])
        rs = sb("rs", [P, 3, 2])
        ytile = sb("ytile", [P, 3, KC, P])
        zh = sb("zh", [P, 3, C])
        area = sb("area", [P, KX * C + XS * KX * P + NPT * C])
        wt = area[:, 0:KX * C].rearrange("p (k n) -> p k n", k=KX)
        xin = area[:, KX * C:KX * C + XS * KX * P].rearrange("p (s k n) -> p s k n", s=XS, k=KX)
        posb = area[:, KX * C + XS * KX * P:].rearrange("p (j n) -> p j n", j=NPT)
        at = 0

        def piece(rows, dims):
            nonlocal at
            n = int(np.prod(dims))
            flat = area[0:rows, at:at + n]
            at += n
            names = " ".join("abcd"[:len(dims)])
            return flat.rearrange(f"p ({names}) -> p {names}", **dict(zip("abcd", dims)))

        kblk = piece(P, (KC, 2, HQ, TP))
        dif = piece(TP, (KC, 2, HQ, TP))
        prob = piece(TP, (KC, 2, HQ, TP))
        qs = piece(P, (2, KC, TP))
        vs = piece(TP, (2, HEADS, VS))
        yraw = piece(P, (KC, 2, TP))
        mx = sb("mx", [TP, KC, 2, HQ])
        rc = sb("rc", [TP, HEADS])
        yn = sb("yn", [TP, C])
        zbn = sb("zbn", [P, KC, B])
        ones_row = sb("ones_row", [1, B])
        top = sb("top", [B, 8])
        ntop = sb("ntop", [B, 1])
        ex = sb("ex", [B, EXPERTS])
        exs = sb("exs", [B, 1])
        exr = sb("exr", [B, 1])
        pr = sb("pr", [B, EXPERTS])
        ptop = sb("ptop", [B, 8])
        pidx = sb("pidx", [B, 8], U32)
        gate_col = sb("gate_col", [B, P])
        idx_col = sb("idx_col", [B, 1])
        gate = sb("gate", [P, B])
        table_probe = sb("table_probe", [1, 1])
        idx = sb("idx", [1, B], I32)
        ps = ctx.enter_context(nc.psum_tensor("ps", [P, 8, 512], F32))

        l_pos, l_pos_rest, l_tokb, l_cls = (sem(n) for n in
                                                   ("l_pos", "l_pos_rest", "l_tokb", "l_cls"))
        l_first = [sem(f"l_first{h}") for h in range(3)]
        l_txt = [sem(f"l_txt{h}") for h in range(2)]
        l_x = [sem(f"l_x{t}") for t in range(XS)]
        l_wattn, l_wproj, l_cols, l_wall = (sem(n) for n in ("l_wattn", "l_wproj", "l_cols", "l_wall"))
        consts, posb_done, bproj_done = sem("consts"), sem("posb_done"), sem("bproj_done")
        mask_done, vs_ones, hid_ones = sem("mask_done"), sem("vs_ones"), sem("hid_ones")
        patch_mm, h_added, stats_a, aggr_a, sqrt_a, recip_a, norm_a, xpose_a, xT_done, xT_last = (
            sem(n) for n in ("patch_mm", "h_added", "stats_a", "aggr_a", "sqrt_a", "recip_a", "norm_a",
                             "xpose_a", "xT_done", "xT_last"))
        cls_dve, cls_sqrt, cls_x, bn_dve = sem("cls_dve"), sem("cls_sqrt"), sem("cls_x"), sem("bn_dve")
        latqv_mm, latk_mm, latqv_cp, latk_cp, v_mm, q_mm, k_mm, q_cp, k_cp, v_cpa, v_cpd = (
            sem(n) for n in ("latqv_mm", "latk_mm", "latqv_cp", "latk_cp", "v_mm", "q_mm", "k_mm", "q_cp",
                             "k_cp", "v_cpa", "v_cpd"))
        qs_done, kblk_done, vs_done, score_mm, max_done, sub_done, prob_xp, exp_done = (
            sem(n) for n in ("qs_done", "kblk_done", "vs_done", "score_mm", "max_done", "sub_done",
                             "prob_xp", "exp_done"))
        pv_mm, yraw_cp, yraw_xp, rec_done, ynorm, yT_xp, yT_cp = (
            sem(n) for n in ("pv_mm", "yraw_cp", "yraw_xp", "rec_done", "ynorm", "yT_xp", "yT_cp"))
        ytile_cp, proj_mm, h1_done, stats_c, aggr_c, sqrt_c, recip_c, zh_done, xpose_c, zT_cp, res_moved = (
            sem(n) for n in ("ytile_cp", "proj_mm", "h1_done", "stats_c", "aggr_c", "sqrt_c", "recip_c",
                             "zh_done", "xpose_c", "zT_cp", "res_moved"))
        r_dve, r_act, r_logit, r_bcast = sem("r_dve"), sem("r_act"), sem("r_logit"), sem("r_bcast")
        wsel_even, wsel_odd, down_mm, relu_done, up_mm, out_done, stored = (
            sem(n) for n in ("wsel_even", "wsel_odd", "down_mm", "relu_done", "up_mm", "out_done", "stored"))

        FILLED, IDENTITIES, PADDING = 7, 9, 16

        PROJ, XP = (0, 1, 7), (2, 3, 6)
        UP = (2, 3, 6, 7)

        LOADED = 8

        def load_experts(engine, start, stop):
            _, values = nc.values_load_multi_w_load_instructions(
                idx[0:1, start:stop:2], engines=[engine], min_val=0, max_val=EXPERTS - 1,
                skip_runtime_bounds_check_because="the index is cut off at EXPERTS - 1")
            return dict(zip(range(start, stop, 2), values))

        block = ctx.enter_context(nc.Block())

        @block.sync
        def _(sp):
            def load_patch(j, t):
                sp.dma_start(xin[:, t, :, :], patches[j, :, :, :]).then_inc(l_x[t], 16)

            def load_weights():
                sp.dma_start(colp[:, :, :], cols).then_inc(l_cols, 16)
                sp.dma_start(wr[:, :, :], w_router).then_inc(l_cols, 16)
                sp.dma_start(br[:, :], b_router).then_inc(l_cols, 16)
                sp.dma_start(wlqv[:, :, :], w_lat_qv).then_inc(l_wattn, 16)
                sp.dma_start(wlk[:, :, :], w_lat_k).then_inc(l_wattn, 16)
                sp.dma_start(whq[:, :], w_heads_q).then_inc(l_wattn, 16)
                sp.dma_start(whk[:, :], w_heads_k).then_inc(l_wattn, 16)
                sp.dma_start(whv[LAT:P, :], w_heads_v).then_inc(l_wattn, 16)
                sp.dma_start(wp[:, :, :], w_proj).then_inc(l_wproj, 16)
                sp.dma_start(bp[:, :], b_proj).then_inc(l_wproj, 16)

            for h in range(3):
                sp.dma_start(xin[:, 0, 2 * h:2 * h + 2, :], patches[0, :, 2 * h:2 * h + 2, :]).then_inc(l_first[h], 16)
            load_patch(1, 1)
            sp.dma_start(posb[:, 0:3, :], pos_rows[:, 0:3, :]).then_inc(l_pos, 16)
            load_patch(2, 2)
            load_patch(3, 3)
            sp.dma_start(posb[:, 3:NPT, :], pos_rows[:, 3:NPT, :]).then_inc(l_pos_rest, 16)
            for j in range(XS, NPT):
                sp.wait_ge(patch_mm, j - XS + 1)
                load_patch(j, j % XS)
                if j == XS + 1:
                    load_weights()
            sp.dma_start(wall[:, :, :], experts).then_inc(l_wall, 16)
            sp.wait_ge(h1_done, 1)
            sp.dma_start(res[0:1, :, :], h0c[:, :]).then_inc(res_moved, 16)
            for n in range(1, NT + 1):
                at = (n - 1) * RT + 1
                sp.wait_ge(h1_done, n + 1)
                sp.dma_start(res[at:at + RT, :, :], h0[:, n - 1, :]).then_inc(res_moved, 16)
            with sp.Fori(0, NG) as i:
                sp.wait_ge(out_done, i * G + G)
                sp.dma_start(out[ds(i * G, G), :, :].rearrange("b t n -> t b n"), res[0:T, ds(i * G, G), :])\
                    .then_inc(stored, 16)
            sp.wait_ge(stored, 16 * NG)

        @block.gpsimd
        def _(pool):
            pool.memset(ident[:, :], 0.0).then_inc(consts, 1)
            pool.memset(ident_bf[:, :], 0.0).then_inc(consts, 1)
            pool.memset(head_of_row[:, :], 1.0).then_inc(consts, 1)
            pool.memset(seq_of_row[:, :], 0.0).then_inc(consts, 1)
            pool.memset(eps_col[:, :], EPS).then_inc(consts, 1)
            pool.memset(eps2_col[:, :], EPS * EPS).then_inc(consts, 1)
            pool.memset(ones_row[:, :], 1.0).then_inc(consts, 1)
            pool.wait_ge(consts, FILLED)
            for m, n in ((ident, P), (ident_bf, TP)):
                pool.affine_select(out=m[:, :], in_=m[:, :], compare_op=ALU.not_equal, fill=1.0, base=0,
                                   pattern=[[-1, n]], channel_multiplier=1).then_inc(consts, 1)
            pool.affine_select(out=head_of_row[:, :], in_=head_of_row[:, :], compare_op=ALU.is_ge, fill=0.0,
                               base=0, pattern=[[-HD, HH]], channel_multiplier=1).then_inc(consts, 1)
            pool.wait_ge(consts, IDENTITIES + 1)
            pool.affine_select(out=head_of_row[:, :], in_=head_of_row[:, :], compare_op=ALU.is_ge, fill=0.0,
                               base=HD - 1, pattern=[[HD, HH]], channel_multiplier=-1).then_inc(consts, 1)
            for r in range(RT):
                pool.affine_select(out=seq_of_row[:, :], in_=seq_of_row[:, :], compare_op=ALU.not_equal, fill=1.0,
                                   base=-B * r, pattern=[[-1, B]], channel_multiplier=1).then_inc(consts, 1)
                pool.wait_ge(consts, IDENTITIES + 3 + r)
            pad = xT[:, :, :].rearrange("p k (b t) -> p k b t", t=TP)[:, :, :, T:TP]
            pool.memset(pad, 0.0).then_inc(consts, 1)
            pool.wait_ge(l_pos, 16)
            pool.wait_ge(l_tokb, 16)
            for j in range(NPT):
                if j == 3:
                    pool.wait_ge(l_pos_rest, 16)
                pool.tensor_tensor(posb[:, j, :], posb[:, j, :], tokb[:, :], ALU.add).then_inc(posb_done, 1)
            pool.memset(mask[:, :, :], 0.0).then_inc(mask_done, 1)
            pool.wait_ge(mask_done, 1)
            pool.affine_select(out=mask[:, :, :], in_=mask[:, :, :], compare_op=ALU.is_ge, fill=NEG, base=0,
                               pattern=[[0, HQ], [-1, TP]], channel_multiplier=1).then_inc(mask_done, 1)
            pool.wait_ge(norm_a, NPT)
            pool.wait_ge(cls_x, 1)
            pool.wait_ge(l_wproj, 16 * 2)
            pool.memset(vs, 1.0).then_inc(vs_ones, 1)
            pool.tensor_tensor(h0[:, :, :], h0[:, :, :], bp[:, :].unsqueeze(1).to_broadcast([P, NT, C]),
                               ALU.add).then_inc(bproj_done, 1)
            pool.tensor_tensor(h0c[:, :], h0c[:, :], bp[0:B, :], ALU.add).then_inc(bproj_done, 1)

            def take_queries(b, t, first=False):
                if not first:
                    pool.wait_ge(score_mm, b * 2 - 2)
                pool.tensor_copy(qs[:, t, :, :], qT[:, :, ds(b * TP, TP)]).then_inc(qs_done, 1)

            def build_kblk(b, f, first=False):
                if not first:
                    pool.wait_ge(score_mm, b * 2 + f - 1)
                pool.tensor_tensor(
                    kblk[:, f, :, :, :].rearrange("p c h k -> p (c h) k"),
                    kT[:, f, ds(b * TP, TP)].unsqueeze(1).to_broadcast([P, HH, TP]),
                    head_of_row[:, :].unsqueeze(2).to_broadcast([P, HH, TP]), ALU.mult).then_inc(kblk_done, 1)

            def take_values(b, t, first=False):
                if not first:
                    pool.wait_ge(pv_mm, b * 2 - 2)
                pool.tensor_copy(vs[:, t, :, 0:HD],
                                 v[:, ds(b, 1), :].rearrange("p o (h d) -> p (o h) d", d=HD))\
                    .then_inc(vs_done, 1)

            pool.wait_ge(patch_mm, NPT)
            pool.wait_ge(q_cp, 1)
            pool.wait_ge(k_cp, 1)
            take_queries(0, 0, first=True)
            take_queries(1, 1, first=True)
            build_kblk(0, 0, first=True)
            build_kblk(0, 1, first=True)
            pool.wait_ge(q_cp, NG)
            pool.wait_ge(k_cp, NG)
            pool.wait_ge(v_cpa, NG)
            pool.wait_ge(v_cpd, NG)
            pool.wait_ge(vs_ones, 1)
            take_values(0, 0, first=True)
            build_kblk(1, 0)
            build_kblk(1, 1)
            take_values(1, 1, first=True)
            with pool.Fori(1, B // 2) as i:
                for t in range(2):
                    b = i * 2 + t
                    take_queries(b, t)
                    build_kblk(b, 0)
                    build_kblk(b, 1)
                    take_values(b, t)

            y4 = yT[:, :, :].rearrange("p k (b t) -> p k b t", t=TP)

            def gather_ytile(n, slot, b0=0, b1=B, done=True):
                cp = pool.tensor_copy(ytile[:, slot, :, :].rearrange("p k (s b) -> p k b s", s=RT)[:, :, b0:b1, :],
                                      y4[:, :, b0:b1, ds(n * RT - RT + 1, RT)])
                if done:
                    cp.then_inc(ytile_cp, 1)

            pool.wait_ge(yT_cp, B - 4)
            for n in range(1, 4):
                gather_ytile(n, n % 3, 0, B - 4, done=False)
            pool.wait_ge(yT_cp, B)
            for n in range(1, 4):
                gather_ytile(n, n % 3, B - 4, B)
            with pool.Fori(1, NT // 3) as i:
                for t in range(3):
                    pool.wait_ge(proj_mm, i * 3 + t - 1)
                    gather_ytile(i * 3 + t + 1, (t + 1) % 3)
            for n in range(NT // 3 * 3 + 1, NT + 1):
                pool.wait_ge(proj_mm, n - 2)
                gather_ytile(n, n % 3)

            pool.wait_ge(l_wall, 16)
            pool.wait_ge(r_dve, 10)

            def pick(b, t):
                e = pool.value_load(idx[0:1, ds(b, 1)], min_val=0, max_val=EXPERTS - 1)
                pool.tensor_copy(wsel[:, t:t + 1, 0:WDN], wall[:, ds(e, 1), 0:WDN]).then_inc(wsel_odd, 1)

            for t in range(1, G, 2):
                pick(t, t)
            with pool.Fori(1, NG) as i:
                for t in range(1, G, 2):
                    pool.wait_ge(relu_done, i * G + t - G + 1)
                    pick(i * G + t, t)

        @block.scalar
        def _(act):
            for h in range(3):
                act.dma_start(wt[:, 2 * h:2 * h + 2, :], wtok[:, 2 * h:2 * h + 2, :]).then_inc(l_first[h], 16)
            act.dma_start(h0c[:, :], cls_tok).then_inc(l_cls, 16)
            act.dma_start(xhc[:, :], pos_cls).then_inc(l_cls, 16)
            act.dma_start(tokb[:, :], tok_b).then_inc(l_tokb, 16)
            act.dma_start(h0[:, NPT:NPT + 2, :], txt[:, 0:2, :]).then_inc(l_txt[0], 16)
            act.dma_start(h0[:, NPT + 2:NT, :], txt[:, 2:NTT, :]).then_inc(l_txt[1], 16)

            x4 = xT[:, :, :].rearrange("p k (b t) -> p k b t", t=TP)

            act.wait_ge(consts, FILLED)
            act.activation(table_probe[:, :], eps_col[0:1, :], ACT.Sqrt)
            act.wait_ge(cls_dve, 3)
            act.activation(sd[0:B, 0, 0:1], mv[0:B, 0, 0, 1:2], ACT.Sqrt, bias=eps_col[0:B, :]).then_inc(cls_sqrt, 1)

            def evac_cls():
                act.wait_ge(xpose_a, 1)
                act.copy(x4[:, :, :, 0:1].rearrange("p k b o -> p k (b o)"),
                         ps[:, 6, 0:KC * B].rearrange("p (k b) -> p k b", k=KC)).then_inc(xT_done, 1)

            def evac_tiles(j, t):
                act.wait_ge(xpose_a, j + 2)
                for u, at in ((0, 1), (1, 1 + NPATCH)):
                    last = act.copy(
                        x4[:, :, :, j * RT + at:(j + 1) * RT + at],
                        ps[:, 3 + t, 2 * u * P:2 * (u + 1) * P].rearrange("p (k s b) -> p k b s", k=KC, s=RT))
                last.then_inc(xT_done, 1)

            def deviations(j, t):
                act.wait_ge(aggr_a, j + 1)
                nu = 2 if j < NTT else 1
                act.activation(sd[:, t, 0:nu], mv[:, t, 0:nu, 1], ACT.Sqrt, bias=eps_col[:, :]).then_inc(sqrt_a, 1)

            for j in range(NPT):
                deviations(j, j % 3)
                if j == 2:
                    evac_cls()
                if j > 2:
                    evac_tiles(j - 3, j % 3)
            for j in range(NPT - 3, NPT - 1):
                evac_tiles(j, j % 3)
            act.wait_ge(bn_dve, 1)
            act.activation(bn_tmp[:, :], bn_scale[:, :], ACT.Sqrt).then_inc(cls_sqrt, 1)

            def latqv_out(g, first=False):
                act.wait_ge(latqv_mm, g + 1)
                if not first:
                    act.wait_ge(q_mm, g)
                act.copy(latqv[:, :], ps[:, 0, 0:GN]).then_inc(latqv_cp, 1)

            def qv_out(g):
                act.wait_ge(v_mm, g * 2 + 2)
                act.copy(v[:, ds(g * G + 2, 2), :],
                         ps[0:TP, 7, :].rearrange("p (b n) -> p b n", b=2)).then_inc(v_cpa, 1)
                act.wait_ge(q_mm, g + 1)
                act.activation(qT[:, :, ds(g * GN, GN)], ps[:, 2:4, 0:GN], ACT.Copy,
                               scale=float(HD) ** -0.5).then_inc(q_cp, 1)

            latqv_out(0, first=True)
            with act.Fori(0, NG - 1) as i:
                act.wait_ge(v_mm, i * 2 + 2)
                act.copy(v[:, ds(i * G + 2, 2), :],
                         ps[0:TP, 7, :].rearrange("p (b n) -> p b n", b=2)).then_inc(v_cpa, 1)
                latqv_out(i + 1)
                act.wait_ge(q_mm, i + 1)
                act.activation(qT[:, :, ds(i * GN, GN)], ps[:, 2:4, 0:GN], ACT.Copy,
                               scale=float(HD) ** -0.5).then_inc(q_cp, 1)
            qv_out(NG - 1)

            def exps(b, f, first=False):
                n = b * 2 + f
                if not first:
                    act.wait_ge(pv_mm, n - 1)
                for c in range(2):
                    act.wait_ge(prob_xp, n * 2 + c + 1)
                    act.activation(prob[:, f, c, :, :].rearrange("p h n -> p (h n)"), ps[0:TP, 4 + c, 0:HC],
                                   ACT.Exp).then_inc(exp_done, 1)

            def yraw_out(b, f, first=False):
                n = b * 2 + f
                act.wait_ge(pv_mm, n + 1)
                if not first:
                    act.wait_ge(yraw_xp, n - 1)
                act.copy(yraw[:, f, :, :].rearrange("p c n -> p (c n)"),
                         ps[:, 6, f * 2 * TP:(f + 1) * 2 * TP]).then_inc(yraw_cp, 1)

            def yT_out(b):
                act.wait_ge(yT_xp, b + 1)
                act.copy(yT[:, :, ds(b * TP, TP)],
                         ps[:, 6, HC:HC + KC * TP].rearrange("p (k n) -> p k n", k=KC)).then_inc(yT_cp, 1)

            act.wait_ge(patch_mm, NPT)
            exps(0, 0, first=True)
            exps(0, 1, first=True)
            yraw_out(0, 0, first=True)
            exps(1, 0)
            yraw_out(0, 1, first=True)
            exps(1, 1)
            yraw_out(1, 0)
            with act.Fori(1, B // 2) as i:
                for t in range(2):
                    b = i * 2 + t
                    exps(b, 0)
                    yraw_out(b - 1, 1)
                    yT_out(b - 2)
                    exps(b, 1)
                    yraw_out(b, 0)
            yraw_out(B - 1, 1)
            yT_out(B - 2)
            yT_out(B - 1)

            z4 = zT[:, :, :].rearrange("p k (b t) -> p k b t", t=TP)

            def deviation_c(n, s, rows):
                act.wait_ge(aggr_c, n + 1)
                act.activation(sd[0:rows, s, 0:1], mv[0:rows, s, 0, 1:2], ACT.Sqrt, bias=eps2_col[0:rows, :],
                               scale=1.0 + EPS).then_inc(sqrt_c, 1)

            def evac_c(n, s, at, cnt):
                act.wait_ge(xpose_c, n + 1)
                for k in range(KC):
                    act.activation(z4[:, k, :, ds(at, cnt)],
                                   ps[:, XP[s], k * B * cnt:(k + 1) * B * cnt].rearrange("p (s b) -> p b s", s=cnt),
                                   ACT.Identity, bias=colp[:, 1, k:k + 1], scale=colp[:, 0, k:k + 1])\
                        .then_inc(zT_cp, 1)

            deviation_c(0, 0, B)
            deviation_c(1, 1, P)
            deviation_c(2, 2, P)
            evac_c(0, 0, 0, 1)
            for n in range(3, 6):
                deviation_c(n, n % 3, P)
                evac_c(n - 2, (n + 1) % 3, (n - 3) * RT + 1, RT)
            with act.Fori(2, (NT + 1) // 3) as i:
                for t in range(3):
                    deviation_c(i * 3 + t, t, P)
                    evac_c(i * 3 + t - 2, (t + 1) % 3, (i * 3 + t) * RT - 3 * RT + 1, RT)
            act.activation(table_probe[:, :], eps_col[0:1, :], ACT.Exp)
            evac_c(NT - 1, (NT - 1) % 3, (NT - 2) * RT + 1, RT)
            act.wait_ge(r_dve, 3)
            act.activation(ex[:, :], ps[0:B, 0, 0:EXPERTS], ACT.Exp, bias=ntop[:, :], accum_out=exs[:, :])\
                .then_inc(r_act, 1)
            evac_c(NT, NT % 3, (NT - 1) * RT + 1, RT)

            act.wait_ge(hid_ones, 2)

            def relu(b, t, first=False):
                act.wait_ge(down_mm, b + 1)
                if not first:
                    act.wait_ge(up_mm, b - G + 1)
                act.activation(hid[0:HID, t, :], ps[0:HID, t % 2, 0:T], ACT.Relu,
                               bias=wsel[0:HID, t, WDN - 1:WDN]).then_inc(relu_done, 1)

            for b in range(B):
                relu(b, b % G, first=(b < G))

        @block.tensor
        def _(pe):
            def products(j, t, first=False):
                if j:
                    pe.wait_ge(l_x[j % XS], (j // XS + (j % XS > 0)) * 16)
                if not first:
                    pe.wait_ge(h_added, j - 2)
                for k in range(KX):
                    if j == 0 and k % 2 == 0:
                        pe.wait_ge(l_first[k // 2], 32)
                    last = nc.tensor.matmul(ps[:, t, 0:C], xin[:, j % XS, k, :], wt[:, k, :], start=(k == 0),
                                            stop=(k == KX - 1))
                last.then_inc(patch_mm, 1)

            def transposes(j, t, first=False, with_txt=True):
                pe.wait_ge(norm_a, j + 1)
                if not first:
                    pe.wait_ge(xT_done, j - 1)
                for u in range(2 if with_txt else 1):
                    for k in range(KC):
                        c = (2 * u + k) * P
                        last = nc.tensor.transpose(ps[:, 3 + t, c:c + P], xh[:, t, u, k * P:(k + 1) * P],
                                                   ident[:, :])
                last.then_inc(xpose_a, 1)

            for j in range(NPT):
                products(j, j % 3, first=(j < 3))
                if j == 2:
                    pe.wait_ge(consts, IDENTITIES)
                    pe.wait_ge(cls_x, 1)
                    for k in range(KC):
                        last = nc.tensor.transpose(ps[:, 6, k * B:(k + 1) * B], xhc[:, k * P:(k + 1) * P],
                                                   ident[0:B, 0:B])
                    last.then_inc(xpose_a, 1)
                if j > 2:
                    transposes(j - 3, j % 3, first=(j < 6))
            for j in range(NPT - 3, NPT - 1):
                transposes(j, j % 3)
            transposes(NPT - 1, (NPT - 1) % 3, with_txt=False)

            def latents(g, first=False):
                cols_ = ds(g * GN, GN)
                if not first:
                    pe.wait_ge(latqv_cp, g)
                for k in range(KC):
                    last = nc.tensor.matmul(ps[:, 0, 0:GN], wlqv[:, k, :], xT[:, k, cols_], start=(k == 0),
                                            stop=(k == KC - 1))
                last.then_inc(latqv_mm, 1)
                if not first:
                    pe.wait_ge(latk_cp, g)
                for k in range(KC):
                    last = nc.tensor.matmul(ps[:, 1, 0:GN], wlk[:, k, :], xT[:, k, cols_], start=(k == 0),
                                            stop=(k == KC - 1))
                last.then_inc(latk_mm, 1)

            def heads(g, first=False):
                pe.wait_ge(latqv_cp, g + 1)
                for u in range(2):
                    if not first:
                        pe.wait_ge((v_cpd, v_cpa)[u], g)
                    for w in range(2):
                        s = 2 * u + w
                        last = nc.tensor.matmul(ps[0:TP, 6 + u, w * C:(w + 1) * C],
                                                latqv[LAT:P, s * TP:(s + 1) * TP], whv[LAT:P, :],
                                                start=True, stop=True)
                    last.then_inc(v_mm, 1)
                if not first:
                    pe.wait_ge(q_cp, g)
                for k in range(KC):
                    last = nc.tensor.matmul(ps[:, 2 + k, 0:GN], whq[:, k * P:(k + 1) * P], latqv[0:LAT, :],
                                            start=True, stop=True)
                last.then_inc(q_mm, 1)
                pe.wait_ge(latk_cp, g + 1)
                if not first:
                    pe.wait_ge(k_cp, g)
                for k in range(KC):
                    last = nc.tensor.matmul(ps[:, 4 + k, 0:GN], whk[:, k * P:(k + 1) * P], latk[0:LAT, :],
                                            start=True, stop=True)
                last.then_inc(k_mm, 1)

            pe.wait_ge(l_wattn, 16 * 5)
            pe.wait_ge(xT_done, NPT)
            pe.wait_ge(xT_last, 1)
            pe.wait_ge(consts, PADDING)
            latents(0, first=True)
            latents(1)
            heads(0, first=True)
            with pe.Fori(1, NG - 1) as i:
                latents(i + 1)
                heads(i)
            heads(NG - 1)

            def scores(b, f, t, first=False, between=None):
                n = b * 2 + f
                if f == 0:
                    pe.wait_ge(qs_done, b + 1)
                pe.wait_ge(kblk_done, n + 1)
                if not first:
                    pe.wait_ge(sub_done, n - 1)
                for c in range(2):
                    bank = ps[0:TP, 2 * f + c, 0:HC]
                    nc.tensor.matmul(bank, ident_bf[:, :], mask[:, :, :].rearrange("p h k -> p (h k)"),
                                     start=True, stop=False)
                    last = nc.tensor.matmul(bank, qs[:, t, f, :],
                                            kblk[:, f, c, :, :].rearrange("p h k -> p (h k)"), start=False,
                                            stop=True)
                    if c == 0 and between:
                        between()
                last.then_inc(score_mm, 1)

            def prob_transposes(b, f, first=False):
                n = b * 2 + f
                pe.wait_ge(sub_done, n + 1)
                for c in range(2):
                    if not first:
                        pe.wait_ge(exp_done, n * 2 - 1 + c)
                    for h in range(HQ):
                        last = nc.tensor.transpose(ps[0:TP, 4 + c, h * TP:(h + 1) * TP], dif[:, f, c, h, :],
                                                   ident[0:TP, 0:TP])
                    last.then_inc(prob_xp, 1)

            def weighted_values(b, f, t, first=False, after_y=False):
                n = b * 2 + f
                pe.wait_ge(exp_done, n * 2 + 2)
                if f == 0:
                    pe.wait_ge(vs_done, b + 1)
                if not first:
                    pe.wait_ge(yraw_cp, n)
                if after_y:
                    pe.wait_ge(yT_cp, b - 1)
                for c in range(2):
                    for h in range(HQ):
                        last = nc.tensor.matmul(ps[h * VS:(h + 1) * VS, 6, (2 * f + c) * TP:(2 * f + c + 1) * TP],
                                                vs[:, t, f * HH + c * HQ + h, :], prob[:, f, c, h, :],
                                                start=True, stop=True, tile_position=(0, h * VS),
                                                skip_group_check=True)
                last.then_inc(pv_mm, 1)

            def yraw_transposes(b, f, first=False):
                n = b * 2 + f
                pe.wait_ge(yraw_cp, n + 1)
                if not first:
                    pe.wait_ge(ynorm, b)
                for c in range(2):
                    at = (2 * f + c) * P
                    last = nc.tensor.transpose(ps[0:TP, 7, at:at + P], yraw[:, f, c, :], ident[:, :])
                last.then_inc(yraw_xp, 1)

            def y_transposes(b, last=False):
                pe.wait_ge(ynorm, b + 1)
                pe.wait_ge(yraw_cp, b * 2 + (2 if last else 4))
                for k in range(KC):
                    done = nc.tensor.transpose(ps[:, 6, HC + k * TP:HC + (k + 1) * TP],
                                               yn[:, k * P:(k + 1) * P], ident[0:TP, 0:TP])
                done.then_inc(yT_xp, 1)

            def attend(b, t, end=False):
                early = b if isinstance(b, int) else 4
                scores(b, 1, t, first=(early == 0))
                prob_transposes(b, 0, first=(early == 0))
                if early > 0:
                    weighted_values(b - 1, 1, 1 - t)
                    yraw_transposes(b - 1, 0, first=(early == 1))
                turn_y = (lambda: y_transposes(b - 2)) if early > 1 else None
                if not end:
                    scores(b + 1, 0, 1 - t, between=turn_y)
                elif turn_y:
                    turn_y()
                prob_transposes(b, 1)
                weighted_values(b, 0, t, first=(early == 0), after_y=(early > 1))
                if early > 0:
                    yraw_transposes(b - 1, 1, first=(early == 1))

            pe.wait_ge(mask_done, 2)
            pe.wait_ge(latqv_cp, NG)
            pe.wait_ge(latk_cp, NG)
            scores(0, 0, 0, first=True)
            pe.wait_ge(q_cp, NG)
            pe.wait_ge(k_cp, NG)
            pe.wait_ge(v_cpa, NG)
            pe.wait_ge(v_cpd, NG)
            for b in range(4):
                attend(b, b % 2)
            with pe.Fori(1, B // 4 - 1) as i:
                for t in range(4):
                    attend(i * 4 + t, t % 2)
            for b in range(B - 4, B):
                attend(b, b % 2, end=(b + 1 == B))
            weighted_values(B - 1, 1, 1)
            yraw_transposes(B - 1, 0)
            y_transposes(B - 2)
            yraw_transposes(B - 1, 1)
            pe.wait_ge(yT_cp, B - 1)
            y_transposes(B - 1, last=True)

            y4 = yT[:, :, :].rearrange("p k (b t) -> p k b t", t=TP)

            def project(n, s, cls=False):
                rows = B if cls else P
                if not cls:
                    pe.wait_ge(ytile_cp, n)
                for k in range(KC):
                    lhsT = y4[:, k, :, 0] if cls else ytile[:, s, k, :]
                    last = nc.tensor.matmul(ps[0:rows, PROJ[s], 0:C], lhsT, wp[:, k, :], start=(k == 0),
                                            stop=(k == KC - 1))
                last.then_inc(proj_mm, 1)

            def ln2_out(n, s, cls=False, end=False):
                rows = B if cls else P
                pe.wait_ge(zh_done, n + 1)
                for k in range(KC):
                    nc.tensor.transpose(ps[:, XP[s], k * rows:(k + 1) * rows], zh[0:rows, s, k * P:(k + 1) * P],
                                        ident[0:rows, 0:rows])
                for k in range(KC):
                    for q in range(HQ):
                        c = k * P + q * VS
                        last = nc.tensor.matmul(ps[q * VS:(q + 1) * VS, 4 + k, 0:B], zh[0:rows, s, c:c + VS],
                                                ident[0:B, 0:B] if cls else seq_of_row[:, :], start=cls, stop=end,
                                                tile_position=(0, q * VS), skip_group_check=True)
                last.then_inc(xpose_c, 1)

            pe.wait_ge(yT_cp, B)
            pe.wait_ge(l_wproj, 32)
            project(0, 0, cls=True)
            project(1, 1)
            project(2, 2)

            def out_step(n, s, first=False):
                pe.wait_ge(h1_done, n - 2)
                project(n, s)
                if not first:
                    pe.wait_ge(zT_cp, n * 2 - 10)
                ln2_out(n - 3, s, cls=isinstance(n, int) and n == 3)

            for n in range(3, 6):
                out_step(n, n % 3, first=True)
            with pe.Fori(2, (NT + 1) // 3) as i:
                for t in range(3):
                    out_step(i * 3 + t, t)
            for n in range(NT - 2, NT + 1):
                pe.wait_ge(zT_cp, n * 2 - 4)
                ln2_out(n, n % 3, end=(n == NT))

            pe.wait_ge(r_dve, 1)
            for k in range(KC):
                nc.tensor.matmul(ps[0:B, 0, 0:EXPERTS], zbn[:, k, :], wr[:, k, :], start=(k == 0), stop=False)
            nc.tensor.matmul(ps[0:B, 0, 0:EXPERTS], ones_row[:, :], br[:, :], start=False, stop=True)\
                .then_inc(r_logit, 1)
            pe.wait_ge(r_dve, 9)
            nc.tensor.matmul(ps[:, 4, 0:B], gate_col[:, :], ident[0:B, 0:B], start=True, stop=True)
            nc.tensor.matmul(ps[0:1, 5, 0:B], idx_col[:, :], ident[0:B, 0:B], start=True, stop=True)\
                .then_inc(r_bcast, 1)

            def down(b, t):
                for k in range(KC):
                    last = nc.tensor.matmul(ps[0:HID, t % 2, 0:T], wsel[:, t, k * HID:(k + 1) * HID],
                                            zT[:, k, ds(b * TP, T)], start=(k == 0), stop=(k == KC - 1))
                last.then_inc(down_mm, 1)

            def up(b, t):
                if b % 2:
                    w_up = wall[:, ds(chosen[b], 1), WDN:WPK].rearrange("p o n -> p (o n)")
                else:
                    w_up = wsel[:, t, WDN:WPK]
                if b >= len(UP):
                    pe.wait_ge(out_done, b - len(UP) + 1)
                pe.wait_ge(relu_done, b + 1)
                nc.tensor.matmul(ps[0:T, UP[t], 0:C], hid[:, t, :], w_up, start=True, stop=True)\
                    .then_inc(up_mm, 1)

            pe.wait_ge(zT_cp, KC * (NT + 1))
            pe.wait_ge(r_dve, 10)
            chosen = {}
            for b in range(B + 2):
                if b < B and b % LOADED == 0:
                    chosen |= load_experts(mybir.EngineType.PE, b + 1, b + LOADED)
                if b > 1:
                    up(b - 2, (b - 2) % G)
                if b < B:
                    pe.wait_ge((wsel_even, wsel_odd)[b % 2], b // 2 + 1)
                    down(b, b % G)

        @block.vector
        def _(dve):
            nc.vector.memset(hid[HID:P, :, :], 0.0).then_inc(hid_ones, 1)
            dve.wait_ge(hid_ones, 1)
            nc.vector.memset(hid[HID:HID + 1, :, :], 1.0).then_inc(hid_ones, 1)
            dve.wait_ge(l_cls, 32)
            nc.vector.tensor_tensor(h0c[:, :], h0c[:, :], xhc[:, :], ALU.add).then_inc(cls_dve, 1)
            dve.wait_ge(cls_dve, 1)
            nc.vector.bn_stats(st[0:B, 0, 0, :], h0c[:, :]).then_inc(cls_dve, 1)
            dve.wait_ge(cls_dve, 2)
            nc.vector.bn_aggr(mv[0:B, 0, 0, :], st[0:B, 0, 0, :]).then_inc(cls_dve, 1)
            dve.wait_ge(cls_sqrt, 1)
            nc.vector.reciprocal(rs[0:B, 0, 0:1], sd[0:B, 0, 0:1]).then_inc(cls_dve, 1)
            dve.wait_ge(cls_dve, 4)
            nc.vector.tensor_scalar(xhc[:, :], h0c[:, :], mv[0:B, 0, 0, 0:1], rs[0:B, 0, 0:1], ALU.subtract,
                                    ALU.mult).then_inc(cls_x, 1)

            def ln1(j, t, first=False, with_txt=True):
                nu = 2 if with_txt else 1
                dve.wait_ge(posb_done, j + 1)
                dve.wait_ge(patch_mm, j + 1)
                nc.vector.tensor_tensor(h0[:, j, :], ps[:, t, 0:C], posb[:, j, :], ALU.add).then_inc(h_added, 1)
                if with_txt:
                    if j in (0, 2):
                        dve.wait_ge(l_txt[j // 2], 16)
                    nc.vector.bn_stats(st[:, t, 1, :], h0[:, j + NPT, :])
                dve.wait_ge(h_added, j + 1)
                nc.vector.bn_stats(st[:, t, 0, :], h0[:, j, :]).then_inc(stats_a, 1)
                dve.wait_ge(stats_a, j + 1)
                for u in range(nu):
                    last = nc.vector.bn_aggr(mv[:, t, u, :], st[:, t, u, :])
                last.then_inc(aggr_a, 1)
                dve.wait_ge(sqrt_a, j + 1)
                nc.vector.reciprocal(rs[:, t, 0:nu], sd[:, t, 0:nu]).then_inc(recip_a, 1)
                dve.wait_ge(recip_a, j + 1)
                if not first:
                    dve.wait_ge(xpose_a, j - 1)
                for u in range(nu):
                    last = nc.vector.tensor_scalar(xh[:, t, u, :], h0[:, j + u * NPT, :], mv[:, t, u, 0:1], rs[:, t, u:u + 1],
                                                   ALU.subtract, ALU.mult)
                last.then_inc(norm_a, 1)

            dve.wait_ge(cls_x, 1)
            for j in range(NPT):
                ln1(j, j % 3, first=(j < 3), with_txt=(j < NTT))
            dve.wait_ge(xpose_a, NPT + 1)
            last_at = (NPT - 1) * RT + 1
            nc.vector.tensor_copy(
                xT[:, :, :].rearrange("p k (b t) -> p k b t", t=TP)[:, :, :, last_at:last_at + RT],
                ps[:, 3 + (NPT - 1) % 3, 0:KC * P].rearrange("p (k s b) -> p k b s", k=KC, s=RT))\
                .then_inc(xT_last, 1)
            dve.wait_ge(l_cols, 48)
            nc.vector.tensor_scalar(bn_scale[:, :], colp[:, 5, :], EPS, None, ALU.add).then_inc(bn_dve, 1)

            def latk_out(g, first=False):
                dve.wait_ge(latk_mm, g + 1)
                if not first:
                    dve.wait_ge(k_mm, g)
                nc.vector.tensor_copy(latk[0:LAT, :], ps[0:LAT, 1, 0:GN]).then_inc(latk_cp, 1)

            def v_out(g):
                dve.wait_ge(v_mm, g * 2 + 1)
                nc.vector.tensor_copy(v[:, ds(g * G, 2), :],
                                      ps[0:TP, 6, :].rearrange("p (b n) -> p b n", b=2))\
                    .then_inc(v_cpd, 1)

            def k_out(g):
                dve.wait_ge(k_mm, g + 1)
                nc.vector.tensor_copy(kT[:, :, ds(g * GN, GN)], ps[:, 4:6, 0:GN]).then_inc(k_cp, 1)

            latk_out(0, first=True)
            dve.wait_ge(cls_sqrt, 2)
            nc.vector.reciprocal(bn_scale[:, :], bn_tmp[:, :]).then_inc(bn_dve, 1)
            dve.wait_ge(bn_dve, 2)
            nc.vector.tensor_tensor(bn_scale[:, :], bn_scale[:, :], colp[:, 2, :], ALU.mult).then_inc(bn_dve, 1)
            nc.vector.tensor_tensor(zs_shift[:, :], colp[:, 1, :], colp[:, 4, :], ALU.subtract).then_inc(bn_dve, 1)
            dve.wait_ge(bn_dve, 4)
            nc.vector.scalar_tensor_tensor(zs_scale[:, :], bn_scale[:, :], 1.0 / T, colp[:, 0, :], ALU.mult,
                                           ALU.mult).then_inc(bn_dve, 1)
            nc.vector.tensor_tensor(bn_tmp[:, :], zs_shift[:, :], bn_scale[:, :], ALU.mult).then_inc(bn_dve, 1)
            dve.wait_ge(bn_dve, 6)
            nc.vector.tensor_tensor(zs_shift[:, :], bn_tmp[:, :], colp[:, 3, :], ALU.add).then_inc(bn_dve, 1)
            with dve.Fori(0, NG - 1) as i:
                v_out(i)
                latk_out(i + 1)
                k_out(i)
            v_out(NG - 1)
            k_out(NG - 1)

            def shift(b, f, first=False):
                n = b * 2 + f
                scores_ = ps[0:TP, 2 * f:2 * f + 2, 0:HC].rearrange("p c (h k) -> p c h k", k=TP)
                dve.wait_ge(score_mm, n + 1)
                nc.vector.tensor_reduce(mx[:, f, :, :], scores_, AX_X, ALU.max).then_inc(max_done, 1)
                dve.wait_ge(max_done, n + 1)
                if not first:
                    dve.wait_ge(prob_xp, n * 2 - 2)
                nc.vector.tensor_tensor(dif[:, f, :, :, :], scores_,
                                        mx[:, f, :, :].unsqueeze(3).to_broadcast([TP, 2, HQ, TP]),
                                        ALU.subtract).then_inc(sub_done, 1)

            def normalise(b, first=False):
                o = ps[0:TP, 7, :].rearrange("p (h d) -> p h d", d=VS)
                dve.wait_ge(yraw_xp, b * 2 + 2)
                nc.vector.reciprocal(rc[:, :], o[:, :, HD]).then_inc(rec_done, 1)
                dve.wait_ge(rec_done, b + 1)
                if not first:
                    dve.wait_ge(yT_xp, b)
                nc.vector.tensor_tensor(yn[:, :].rearrange("p (h d) -> p h d", d=HD), o[:, :, 0:HD],
                                        rc[:, :].unsqueeze(2).to_broadcast([TP, HEADS, HD]), ALU.mult)\
                    .then_inc(ynorm, 1)

            dve.wait_ge(patch_mm, NPT)
            for b in range(4):
                shift(b, 0, first=(b == 0))
                if b > 1:
                    normalise(b - 2, first=(b == 2))
                shift(b, 1, first=(b == 0))
            with dve.Fori(1, B // 4) as i:
                for t in range(4):
                    b = i * 4 + t
                    shift(b, 0)
                    normalise(b - 2)
                    shift(b, 1)
            normalise(B - 2)
            normalise(B - 1)

            def tile(n, cls):
                return h0c[:, :] if cls else h0[:, ds(n - 1, 1), :].rearrange("p o n -> p (o n)")

            def add_residual(n, s, cls=False):
                rows = B if cls else P
                dve.wait_ge(proj_mm, n + 1)
                nc.vector.tensor_tensor(tile(n, cls), ps[0:rows, PROJ[s], 0:C], tile(n, cls), ALU.add)\
                    .then_inc(h1_done, 1)

            def take_stats(n, s, cls=False):
                nc.vector.bn_stats(st[0:B if cls else P, s, 0, :], tile(n, cls)).then_inc(stats_c, 1)

            def merge_stats(s, rows=P):
                nc.vector.bn_aggr(mv[0:rows, s, 0, :], st[0:rows, s, 0, :]).then_inc(aggr_c, 1)

            def invert(n, s, cls=False):
                rows = B if cls else P
                dve.wait_ge(sqrt_c, n + 1)
                nc.vector.reciprocal(rs[0:rows, s, 0:1], sd[0:rows, s, 0:1]).then_inc(recip_c, 1)

            def standardise(n, s, cls=False):
                rows = B if cls else P
                dve.wait_ge(recip_c, n + 1)
                nc.vector.tensor_scalar(zh[0:rows, s, :], tile(n, cls), mv[0:rows, s, 0, 0:1],
                                        rs[0:rows, s, 0:1], ALU.subtract, ALU.mult).then_inc(zh_done, 1)

            def ln2_step(n, s):
                fixed = isinstance(n, int)
                dve.wait_ge(stats_c, n)
                add_residual(n, s)
                merge_stats((s + 2) % 3, B if fixed and n == 1 else P)
                dve.wait_ge(h1_done, n + 1)
                if not fixed or n > 1:
                    if not fixed or n > 4:
                        dve.wait_ge(xpose_c, n - 4)
                    standardise(n - 2, (s + 1) % 3, fixed and n == 2)
                take_stats(n, s)
                invert(n - 1, (s + 2) % 3, fixed and n == 1)

            dve.wait_ge(bproj_done, 2)
            add_residual(0, 0, cls=True)
            dve.wait_ge(h1_done, 1)
            take_stats(0, 0, cls=True)
            for n in range(1, NT + 1):
                ln2_step(n, n % 3)
            dve.wait_ge(stats_c, NT + 1)
            merge_stats(NT % 3)
            dve.wait_ge(xpose_c, NT - 3)
            standardise(NT - 1, (NT - 1) % 3)
            invert(NT, NT % 3)
            dve.wait_ge(xpose_c, NT - 2)
            standardise(NT, NT % 3)

            dve.wait_ge(xpose_c, NT + 1)
            for k in range(KC):
                last = nc.vector.tensor_scalar(zbn[:, k, :], ps[:, 4 + k, 0:B], zs_scale[:, k:k + 1],
                                               zs_shift[:, k:k + 1], ALU.mult, ALU.add)
            last.then_inc(r_dve, 1)
            dve.wait_ge(r_logit, 1)
            nc.vector.max(top[:, :], ps[0:B, 0, 0:EXPERTS]).then_inc(r_dve, 1)
            dve.wait_ge(r_dve, 2)
            nc.vector.tensor_scalar(ntop[:, :], top[:, 0:1], -1.0, None, ALU.mult).then_inc(r_dve, 1)
            dve.wait_ge(r_act, 1)
            nc.vector.reciprocal(exr[:, :], exs[:, :]).then_inc(r_dve, 1)
            dve.wait_ge(r_dve, 4)
            nc.vector.tensor_scalar(pr[:, :], ex[:, :], exr[:, 0:1], None, ALU.mult).then_inc(r_dve, 1)
            dve.wait_ge(r_dve, 5)
            nc.vector.max(ptop[:, :], pr[:, :]).then_inc(r_dve, 1)
            dve.wait_ge(r_dve, 6)
            nc.vector.max_index(pidx[:, :], ptop[:, :], pr[:, :]).then_inc(r_dve, 1)
            dve.wait_ge(r_dve, 7)
            nc.vector.tensor_scalar(idx_col[:, :], pidx[:, 0:1], float(EXPERTS - 1), None, ALU.min)\
                .then_inc(r_dve, 1)
            nc.vector.tensor_copy(gate_col[:, :], ptop[:, 0:1].to_broadcast([B, P])).then_inc(r_dve, 1)
            dve.wait_ge(r_bcast, 1)
            nc.vector.tensor_copy(idx[:, :], ps[0:1, 5, 0:B]).then_inc(r_dve, 1)
            nc.vector.tensor_copy(gate[:, :], ps[:, 4, 0:B]).then_inc(r_dve, 1)

            def finish(b, t):
                dve.wait_ge(up_mm, b + 1)
                row = res[0:T, ds(b, 1), :].rearrange("p o n -> p (o n)")
                nc.vector.scalar_tensor_tensor(row, ps[0:T, UP[t], 0:C], gate[0:T, ds(b, 1)], row, ALU.mult,
                                               ALU.add).then_inc(out_done, 1)

            picked = {}
            def pick(b, t):
                if b % LOADED == 0:
                    picked.update(load_experts(mybir.EngineType.DVE, b, b + LOADED))
                nc.vector.tensor_copy(wsel[:, t:t + 1, :], wall[:, ds(picked[b], 1), :]).then_inc(wsel_even, 1)

            dve.wait_ge(r_dve, 11)
            dve.wait_ge(l_wall, 16)
            pick(0, 0)
            pick(2, 2)
            dve.wait_ge(res_moved, 16 * (NT + 1))
            for b in range(B):
                finish(b, b % G)
                if b % 2 == 0 and b + G < B:
                    pick(b + G, b % G)


_OUT = (B, T, C)


def kernel(**inputs):
    import concourse.bacc as bacc
    from concourse.bass_utils import run_bass_kernel_spmd as run

    a = {k: np.asarray(v) for k, v in inputs.items()}
    con = np.ascontiguousarray

    x = a["x"].reshape(B, 3, 6, 16, 6, 16).transpose(0, 2, 4, 1, 3, 5).reshape(B, NPT, RT, KX, P)
    patches = x.transpose(1, 4, 3, 2, 0).reshape(NPT, P, KX, P)
    tiled = lambda w: w.reshape(-1, P, w.shape[-1]).transpose(1, 0, 2)
    pos = a["L0_tok_pos_embedding"][0]
    pos_rows = np.broadcast_to(pos[1:1 + NPATCH].reshape(NPT, RT, C).transpose(1, 0, 2)[:, None], (RT, B, NPT, C))
    rows = lambda r, n: np.broadcast_to(r.reshape(1, -1), (n, r.size))
    col = lambda r: r.reshape(KC, P).T
    up_ = np.zeros((EXPERTS, P, C), np.float32)
    up_[:, 0:HID] = a["L0_ffn_W_up"]
    up_[:, HID] = a["L0_ffn_b_up"]
    bd = np.zeros((EXPERTS, P, 1), np.float32)
    bd[:, 0:HID, 0] = a["L0_ffn_b_down"]
    down_ = a["L0_ffn_W_down"].reshape(EXPERTS, KC, P, HID).transpose(0, 2, 1, 3).reshape(EXPERTS, P, KC * HID)
    arrays = dict(
        patches=patches, wtok=tiled(a["L0_tok_W"].T),
        txt=a["txt"].reshape(B, NTT, RT, C).transpose(2, 0, 1, 3).reshape(P, NTT, C),
        pos_rows=pos_rows.reshape(P, NPT, C), tok_b=rows(a["L0_tok_b"], P),
        cls_tok=rows(a["L0_tok_class_token"], B), pos_cls=rows(pos[0], B),
        w_lat_qv=tiled(np.concatenate([a["L0_attn_wq_lat"], a["L0_attn_wv_lat"]], 1)),
        w_lat_k=tiled(np.concatenate([a["L0_attn_wk_lat"]] * 2, 1)), w_heads_q=a["L0_attn_wq_heads"], w_heads_k=a["L0_attn_wk_heads"],
        w_heads_v=a["L0_attn_wv_heads"], w_proj=tiled(a["L0_attn_w_proj"]), b_proj=rows(a["L0_attn_b_proj"], P),
        cols=np.stack([col(a["L0_ffn_" + n]) for n in ("ln_g", "ln_b", "bn_g", "bn_b", "bn_mean", "bn_var")], 1),
        w_router=tiled(a["L0_ffn_Wr"]), b_router=rows(a["L0_ffn_br"], 1),
        experts=np.concatenate([down_, bd, up_], 2).transpose(1, 0, 2))

    nc = bacc.Bacc("TRN2", target_bir_lowering=False, num_devices=1)
    arrays = {f"in_{k}": con(v) for k, v in arrays.items()}
    args = [nc.dram_tensor(k, v.shape, F32, kind="ExternalInput").ap() for k, v in arrays.items()]
    out = nc.dram_tensor("out_rows", _OUT, F32, kind="ExternalOutput").ap()
    early_fusion(nc, *args, out)
    r = run(nc, [arrays], core_ids=[0])
    return np.asarray(r.results[0]["out_rows"]).reshape(B, T, C)
```
